# Optimizing a Trainium2 kernel written in Bass

```python
import numpy as np
import jax
import jax.numpy as jnp

def _softmax(x, axis=-1):
    return jax.nn.softmax(x, axis=axis)

def _gelu(x):
    return jax.nn.gelu(x, approximate=True)

def _silu(x):
    return jax.nn.silu(x)

def _sigmoid(x):
    return jax.nn.sigmoid(x)

def _layernorm(x, axis=-1, eps=1e-05):
    m = jnp.mean(x, axis=axis, keepdims=True)
    v = jnp.var(x, axis=axis, keepdims=True)
    return (x - m) / jnp.sqrt(v + eps)

def _scatter_add(tgt, idx, src, axis=0):
    return tgt.at[idx].add(src)

def _segment_sum(src, seg, n):
    return jax.ops.segment_sum(src, seg, n)
kernel_name = 'mk_xattn_ffn_d1_seqx_r4_8b3185'

def setup_inputs(seed: int=0):
    np.random.seed(seed)
    _w = jnp.asarray

    def _rec_inputs():
        import jax
        import jax.numpy as jnp
        _rk = jax.random.key(seed)
        x = 7.22e-05 + 1 * jax.random.normal(jax.random.fold_in(_rk, 1), (4, 512, 512), jnp.float32)
        _lenS = 512 - jax.random.randint(jax.random.fold_in(_rk, 7), (4,), 0, max(1, 512 // 4) + 1, jnp.int32)
        _lenS2 = 512 - jax.random.randint(jax.random.fold_in(_rk, 8), (4,), 0, max(1, 512 // 4) + 1, jnp.int32)
        _ctx_512P = jax.random.normal(jax.random.fold_in(_rk, 11), (4, 16, 128), jnp.float32)
        _ctx_512c = jax.random.dirichlet(jax.random.fold_in(_rk, 511), 0.3 * jnp.ones((16,), jnp.float32), (4, 512))
        _ctx_512t = jnp.einsum('bsk,bkd->bsd', _ctx_512c, _ctx_512P)
        _ctx_512t = _ctx_512t * jax.lax.rsqrt(jnp.mean(jnp.square(_ctx_512t)) + 1e-12) * 0.953939
        ctx_512 = -0.000514642 + 1.00011 * (_ctx_512t + 0.3 * jax.random.normal(jax.random.fold_in(_rk, 611), (4, 512, 128), jnp.float32))
        return (x, ctx_512)
    x, ctx_512 = _rec_inputs()

    def _L0_xattn_setup():
        import jax, jax.numpy as jnp
        import numpy as np
        N_HEADS = 16
        N_KV_HEADS = 4
        ROPE_THETA = 10000.0
        EPS = 1e-05

        def _rms_norm(x, w):
            var = jnp.mean(x * x, axis=-1, keepdims=True)
            return x * jax.lax.rsqrt(var + EPS) * w

        def _rope_sin_cos(T, head_dim, dtype):
            inv_freq = 1.0 / ROPE_THETA ** (jnp.arange(0, head_dim, 2, dtype=jnp.float32) / head_dim)
            t = jnp.arange(T, dtype=jnp.float32)
            freqs = jnp.outer(t, inv_freq)
            emb = jnp.concatenate([freqs, freqs], -1)
            return (jnp.sin(emb).astype(dtype)[None, None], jnp.cos(emb).astype(dtype)[None, None])

        def _rotate_half(x):
            h = x.shape[-1] // 2
            x1, x2 = (x[..., :h], x[..., h:])
            return jnp.concatenate([-x2, x1], axis=-1)
        key = jax.random.key(seed)
        ks = jax.random.split(key, 6)
        B, T, C = (2, 512, 512)
        Ckv = C // N_HEADS * N_KV_HEADS
        return {'q': jax.random.normal(ks[0], (B, T, C), jnp.float32), 'k': jax.random.normal(ks[1], (B, T, Ckv), jnp.float32), 'v': jax.random.normal(ks[2], (B, T, Ckv), jnp.float32), 'q_norm_w': jnp.ones((C,), jnp.float32), 'k_norm_w': jnp.ones((Ckv,), jnp.float32), 'w_out': jax.random.normal(ks[3], (C, C), jnp.float32) * C ** (-0.5)}
    _L0_xattn_all = _L0_xattn_setup()
    _L0_xattn_in = {k: v for k, v in _L0_xattn_all.items() if k in ('q_norm_w', 'k_norm_w', 'w_out')}
    del _L0_xattn_all

    def _L0_ffn_setup():
        import jax, jax.numpy as jnp
        import numpy as np
        H = 512
        I = 256
        K = 8
        E = 128
        TOPK = 4
        EPS = 1e-08
        key = jax.random.key(seed)
        ks = jax.random.split(key, 10)
        s = 0.02
        return {'x': jax.random.normal(ks[0], (4, 512, H), jnp.float32), 'w_router': jax.random.normal(ks[1], (H, E), jnp.float32) * s, 'w_gate': jax.random.normal(ks[2], (H, K * I), jnp.float32) * s, 'w_up': jax.random.normal(ks[3], (H, K * I), jnp.float32) * s, 'w_down': jax.random.normal(ks[4], (I, H), jnp.float32) * s, 'amplitudes': jax.random.normal(ks[5], (E, K, 2), jnp.float32) * 0.1, 'expert_scale': jnp.ones((E,), jnp.float32), 'shared_w_gate': jax.random.normal(ks[6], (H, 2 * I), jnp.float32) * s, 'shared_w_up': jax.random.normal(ks[7], (H, 2 * I), jnp.float32) * s, 'shared_w_down': jax.random.normal(ks[8], (2 * I, H), jnp.float32) * s}
    _L0_ffn_all = _L0_ffn_setup()
    _L0_ffn_in = {k: v for k, v in _L0_ffn_all.items() if k in ('w_router', 'w_gate', 'w_up', 'w_down', 'amplitudes', 'expert_scale', 'shared_w_gate', 'shared_w_up', 'shared_w_down')}
    del _L0_ffn_all
    return {'x': x, 'ctx_512': ctx_512, 'L0_xattn_q_norm_w': _L0_xattn_in['q_norm_w'], 'L0_xattn_k_norm_w': _L0_xattn_in['k_norm_w'], 'L0_xattn_w_out': _L0_xattn_in['w_out'], 'L0_ffn_w_router': _L0_ffn_in['w_router'], 'L0_ffn_w_gate': _L0_ffn_in['w_gate'], 'L0_ffn_w_up': _L0_ffn_in['w_up'], 'L0_ffn_w_down': _L0_ffn_in['w_down'], 'L0_ffn_amplitudes': _L0_ffn_in['amplitudes'], 'L0_ffn_expert_scale': _L0_ffn_in['expert_scale'], 'L0_ffn_shared_w_gate': _L0_ffn_in['shared_w_gate'], 'L0_ffn_shared_w_up': _L0_ffn_in['shared_w_up'], 'L0_ffn_shared_w_down': _L0_ffn_in['shared_w_down']}

def reference(x, ctx_512, L0_xattn_q_norm_w, L0_xattn_k_norm_w, L0_xattn_w_out, L0_ffn_w_router, L0_ffn_w_gate, L0_ffn_w_up, L0_ffn_w_down, L0_ffn_amplitudes, L0_ffn_expert_scale, L0_ffn_shared_w_gate, L0_ffn_shared_w_up, L0_ffn_shared_w_down):
    import jax
    import jax.numpy as jnp

    def _L0_xattn_ref(q, k, v, q_norm_w, k_norm_w, w_out):
        import jax, jax.numpy as jnp
        import numpy as np
        N_HEADS = 16
        N_KV_HEADS = 4
        ROPE_THETA = 10000.0
        EPS = 1e-05

        def _rms_norm(x, w):
            var = jnp.mean(x * x, axis=-1, keepdims=True)
            return x * jax.lax.rsqrt(var + EPS) * w

        def _rope_sin_cos(T, head_dim, dtype):
            inv_freq = 1.0 / ROPE_THETA ** (jnp.arange(0, head_dim, 2, dtype=jnp.float32) / head_dim)
            t = jnp.arange(T, dtype=jnp.float32)
            freqs = jnp.outer(t, inv_freq)
            emb = jnp.concatenate([freqs, freqs], -1)
            return (jnp.sin(emb).astype(dtype)[None, None], jnp.cos(emb).astype(dtype)[None, None])

        def _rotate_half(x):
            h = x.shape[-1] // 2
            x1, x2 = (x[..., :h], x[..., h:])
            return jnp.concatenate([-x2, x1], axis=-1)
        B, T, C = q.shape
        hd = C // N_HEADS
        g = N_HEADS // N_KV_HEADS
        q = _rms_norm(q, q_norm_w)
        k = _rms_norm(k, k_norm_w)
        q = q.reshape(B, T, N_HEADS, hd).transpose(0, 2, 1, 3)
        k = k.reshape(B, T, N_KV_HEADS, hd).transpose(0, 2, 1, 3)
        v = v.reshape(B, T, N_KV_HEADS, hd).transpose(0, 2, 1, 3)
        sin, cos = _rope_sin_cos(T, hd, q.dtype)
        q = q * cos + _rotate_half(q) * sin
        k = k * cos + _rotate_half(k) * sin
        qg = q.reshape(B, N_KV_HEADS, g, T, hd)
        scale = 1.0 / jnp.sqrt(jnp.asarray(hd, q.dtype))
        scores = jnp.einsum('bgnqd,bgkd->bgnqk', qg, k) * scale
        causal = jnp.tril(jnp.ones((T, T), bool))
        scores = jnp.where(causal, scores, jnp.asarray(-1e+30, scores.dtype))
        attn = jax.nn.softmax(scores, axis=-1)
        out = jnp.einsum('bgnqk,bgkd->bgnqd', attn, v)
        out = out.reshape(B, N_HEADS, T, hd).transpose(0, 2, 1, 3).reshape(B, T, C)
        return out @ w_out.T

    def _L0_ffn_ref(x, w_router, w_gate, w_up, w_down, amplitudes, expert_scale, shared_w_gate, shared_w_up, shared_w_down):
        import jax, jax.numpy as jnp
        import numpy as np
        H = 512
        I = 256
        K = 8
        E = 128
        TOPK = 4
        EPS = 1e-08
        B, S, _ = x.shape
        T = B * S
        xt = x.reshape(T, H)
        probs = jax.nn.softmax(xt @ w_router, axis=-1)
        topk_p, topk_idx = jax.lax.top_k(probs, TOPK)
        topk_w = topk_p / (jnp.sum(topk_p, axis=-1, keepdims=True) + EPS)
        gate = (xt @ w_gate).reshape(T, K, I)
        up = (xt @ w_up).reshape(T, K, I)
        basis = jax.nn.silu(gate) * up
        p = amplitudes[..., 0] ** 2 + amplitudes[..., 1] ** 2
        mix = p / (jnp.sum(p, axis=-1, keepdims=True) + EPS)
        mix_sel = mix[topk_idx]
        mixed = jnp.einsum('tek,tki->tei', mix_sel, basis)
        down = jnp.einsum('tei,ih->teh', mixed, w_down)
        coeff = topk_w * expert_scale[topk_idx]
        out = jnp.einsum('teh,te->th', down, coeff)
        shared = jax.nn.silu(xt @ shared_w_gate) * (xt @ shared_w_up) @ shared_w_down
        out = out + shared
        return out.reshape(B, S, H)
    x = x + _L0_xattn_ref(_layernorm(x, axis=-1), ctx_512, ctx_512, L0_xattn_q_norm_w, L0_xattn_k_norm_w, L0_xattn_w_out)
    x = x + _L0_ffn_ref(_layernorm(x, axis=-1), L0_ffn_w_router, L0_ffn_w_gate, L0_ffn_w_up, L0_ffn_w_down, L0_ffn_amplitudes, L0_ffn_expert_scale, L0_ffn_shared_w_gate, L0_ffn_shared_w_up, L0_ffn_shared_w_down)
    return x

_drawn_inputs = setup_inputs


def setup_inputs(seed=0):
    import zlib

    import numpy as np

    out = dict(_drawn_inputs(seed))
    spreads = {'L0_xattn_q_norm_w': (1.0, 0.2),
     'L0_xattn_k_norm_w': (1.0, 0.2),
     'L0_ffn_expert_scale': (1.0, 0.6)}
    factors = {'L0_ffn_w_router': 8.0,
     'L0_ffn_w_gate': 4.757,
     'L0_ffn_w_up': 4.648,
     'L0_ffn_w_down': 4.638,
     'L0_ffn_amplitudes': 8.0,
     'L0_ffn_shared_w_gate': 3.042,
     'L0_ffn_shared_w_up': 2.96,
     'L0_ffn_shared_w_down': 2.981}
    for name, (base, spread) in spreads.items():
        noise = np.random.default_rng([zlib.crc32(name.encode()), seed]).standard_normal(out[name].shape)
        drawn = base * np.exp(spread * noise) if base else spread * noise
        out[name] = jnp.asarray(drawn.astype(out[name].dtype))
    for name, factor in factors.items():
        out[name] = (out[name] * factor).astype(out[name].dtype)
    return out
```

```python
import math
from contextlib import ExitStack

import concourse.bass as bass
from concourse import mybir


class Plan:

    def __init__(self):
        self.steps = {"pe": [], "act": [], "dve": [], "pool": [], "sp": []}
        self.reached = {}
        self.sems = {}
        self.waited = {}

    def add(self, lane, name, issue):
        assert name not in self.reached, name
        self.steps[lane].append((issue, True))
        self.reached[name] = (self.sems[lane], sum(marks for _, marks in self.steps[lane]))

    def load(self, name, stream, count, issue):
        assert name not in self.reached, name
        sem, total = self.sems[stream]
        total += 16 * count
        self.sems[stream] = (sem, total)
        self.steps["sp"].append((lambda e, s=sem: issue(e, s), False))
        self.reached[name] = (sem, total)

    def need(self, engine, *names):
        for name in names:
            sem, count = self.reached[name]
            key = (id(engine), id(sem))
            if self.waited.get(key, 0) < count:
                engine.wait_ge(sem, count)
                self.waited[key] = count

    def run(self, lane, engine):
        for issue, marks in self.steps[lane]:
            last = issue(engine)
            if marks:
                last.then_inc(self.sems[lane], 1)


def attention_and_mixture_kernel(nc, x, ctx_in, q_norm_w, k_norm_w, w_out, w_router, w_gate, w_up,
                                 w_down, amplitudes, expert_scale, shared_w_gate, shared_w_up,
                                 shared_w_down, rope_cos, rope_sin, out):
    F32, F32R, BF16, F16, U32 = (mybir.dt.float32, mybir.dt.float32r, mybir.dt.bfloat16,
                                 mybir.dt.float16, mybir.dt.uint32)
    ALU, ACT, AX = mybir.AluOpType, mybir.ActivationFunctionType, mybir.AxisListType
    P = 128
    B, T, C = x.shape
    KVW = ctx_in.shape[2]
    D = rope_cos.shape[1]
    HALF = D // 2
    KV = KVW // D
    G = C // D // KV
    TT = T // P
    NT = B * TT
    KC = C // P
    NC = B * KV
    NH = NC * G
    NE = w_router.shape[1]
    I = w_down.shape[0]
    NK = w_gate.shape[1] // I
    NS = shared_w_gate.shape[1] // I
    NW = NK + NS
    ND = (I + NS * I) // P
    TOPK = 4
    EPS = 1e-5
    EPS_FFN = 1e-8
    SCALE = 1.0 / math.sqrt(D)
    NEG = -1e30
    PBIAS = math.log(256.0)
    PARTS = 3 * D
    VS = PARTS + 2
    MAXROW = 3 * D
    ROWS = MAXROW + 2
    QR, KR = 3, 8
    LEAD = 6
    BASE = [sum(T - P * j for j in range(k)) for k in range(TT)]
    PW = sum(T - P * k for k in range(TT))
    XW = BASE[2]
    YW = PW - XW

    plan = Plan()
    need, add = plan.need, plan.add
    common = ExitStack()
    with common:
        def sb_in(stack):
            return lambda name, shape, dt=F32: stack.enter_context(nc.sbuf_tensor(name, shape, dt))

        sb = sb_in(common)
        x1 = sb("x1", [P, NT, C])
        raw = sb("raw", [P, KC, 2 * I])
        ident = sb("ident", [P, P])
        iota_e = sb("iota_e", [P, NE])
        mixs = sb("mixs", [NE, NK])
        amp = sb("amp", [NE, NK, 2])
        amp_s = sb("amp_s", [NE, NK])
        es = sb("es", [NE, 4])
        cst = sb("cst", [P, 16])
        half_neg = cst[:, 0:8]
        log256 = cst[:, 8:9]

        att_mem = ExitStack()
        sb = sb_in(att_mem)
        cos_t = sb("cos_t", [P, TT, D])
        sin_t = sb("sin_t", [P, TT, D])
        ident16 = sb("ident16", [P, P], BF16)
        mask_kq = sb("mask_kq", [P, P], BF16)
        mask_qk = sb("mask_qk", [P, T])
        junk = sb("junk", [P, TT, KVW], BF16)
        wq_b = sb("wq_b", [P, C])
        wk_b = sb("wk_b", [P, KVW])
        xc = sb("xc", [P, 2, TT, C])
        ct = sb("ct", [P, 2, TT, KVW])
        stats = sb("stats", [P, 2, TT, 6])
        mv = sb("mv", [P, 2, TT, 2])
        ssk = sb("ssk", [P, 2, TT])
        sc = sb("sc", [P, 2, 8, TT])
        csq = sb("csq", [P, 2, 2, 2, TT, D])
        rw_b = sb("rw_b", [P, 2, TT, P])
        r1_b = sb("r1_b", [P, 2, TT, P])
        r2_b = sb("r2_b", [P, TT, P])
        turned_h = sb("turned_h", [P, 2, T], F32R)
        turned_l = sb("turned_l", [P, 2, T], F32R)
        q_st = sb("q_st", [ROWS, QR, G, T], F32R)
        k_st = sb("k_st", [ROWS, KR, T], F32R)
        vp = sb("vp", [P, 2, TT, KV, VS], BF16)
        vr = sb("vr", [P, TT, KVW])
        mx = sb("mx", [P, 2, TT, G])
        mhl = sb("mhl", [P, 2, TT, 2 * G], F32R)
        m_t = sb("m_t", [2 * G, T], F32R)
        p32 = sb("p32", [P, 2, PW])
        p_h = sb("p_h", [P, 2, PW], F16)
        p_l = sb("p_l", [P, 2, PW], F16)
        osb = sb("osb", [P, 2, G, TT, VS])
        rinv = sb("rinv", [P, 2, G, TT])
        att = sb("att", [P, TT, P])
        o_h = sb("o_h", [P, KV, T], F32R)
        o_l = sb("o_l", [P, KV, T], F32R)
        wo_h = sb("wo_h", [P, KC, C], F32R)
        wo_l = sb("wo_l", [P, KC, C], F32R)
        att_mem.close()

        ffn_mem = ExitStack()
        sb = sb_in(ffn_mem)
        t_h = sb("t_h", [P, KC, NT * P], F32R)
        t_l = sb("t_l", [P, KC, NT * P], F32R)
        macc = sb("macc", [P, NT, I])
        w_h = sb("w_h", [P, 2, KC, 2 * I], F32R)
        w_l = sb("w_l", [P, 2, KC, 2 * I], F32R)
        th = sb("th", [P, 2, I])
        ga = sb("ga", [P, 2, I])
        gb = sb("gb", [P, 2, I])
        hs = sb("hs", [P, 2, NS * I])
        wt = sb("wt", [P, NT, NK])
        st2 = sb("st2", [P, 2, 6])
        mv2 = sb("mv2", [P, 2, 2])
        s2 = sb("s2", [P, 2, 4])
        d_h = sb("d_h", [P, 2, ND, P], F32R)
        d_l = sb("d_l", [P, 2, ND, P], F32R)
        wd_h = sb("wd_h", [P, I // P, C], F32R)
        wd_l = sb("wd_l", [P, I // P, C], F32R)
        first_mem = ExitStack()
        sb = sb_in(first_mem)
        rt_w = sb("rt_w", [P, KC, 2 * NE], F32R)
        xn = sb("xn", [P, 2, C])
        lg = sb("lg", [P, 2, NE])
        ex = sb("ex", [P, 2, NE])
        cf = sb("cf", [P, 2, NE])
        cf_t = sb("cf_t", [NE, 2, P])
        sm = sb("sm", [P, 2, 8])
        top = sb("top", [P, 2, 8])
        idx = sb("idx", [P, 2, 8], U32)
        idf = sb("idf", [P, 2, 8])
        first_mem.close()
        last_mem = ExitStack()
        sb = sb_in(last_mem)
        ws_h = sb("ws_h", [P, NS * I // P, C], F32R)
        ws_l = sb("ws_l", [P, NS * I // P, C], F32R)
        last_mem.close()
        ffn_mem.close()

        pair = common.enter_context(nc.psum_tensor("pair", [P, 1024], F32))
        bank = [common.enter_context(nc.psum_tensor(f"bank{i}", [P, 512], F32)) for i in range(6)]
        a_bank = bank[0:2]
        b_bank = bank[2]
        v_bank = bank[3]
        m_bank = bank[4:6]
        g_bank = [pair[:, 0:512], pair[:, 512:1024], bank[0], bank[1]]
        f_bank = [bank[2], bank[3]]
        y_bank = [bank[4], bank[5]]

        def sem(name):
            return common.enter_context(nc.semaphore(name))

        for lane in plan.steps:
            plan.sems[lane] = sem(f"{lane}_done")
        for stream in (["consts", "wo", "amps", "router", "out0", "out1", "raw0", "raw1", "m0", "m1"]
                       + [f"x{t}" for t in range(TT)] + ["x_b1", "c_b0", "c_b1"]
                       + [f"q{i}" for i in range(QR)] + [f"k{i}" for i in range(KR)]):
            plan.sems[stream] = (sem(f"{stream}_landed"), 0)

        f32 = lambda ap: ap.bitcast(F32)

        def constants():
            def masks(e):
                e.memset(log256, PBIAS)
                e.memset(mask_qk[:], 0.0)
                e.memset(ident[:], 0.0)
                e.memset(ident16[:], 0.0)
                e.memset(mask_kq[:], 0.0)
                return e.memset(iota_e[:], 0.0)
            add("pool", "zeroed", masks)

            def shapes(e):
                need(e, "zeroed")
                for m in (ident, ident16):
                    e.affine_select(out=m[:], in_=m[:], compare_op=ALU.not_equal, fill=1.0, base=0,
                                    pattern=[[-1, P]], channel_multiplier=1)
                e.affine_select(out=mask_kq[:], in_=mask_kq[:], compare_op=ALU.is_ge, fill=NEG,
                                base=0, pattern=[[1, P]], channel_multiplier=-1)
                tri = mask_qk[:, T - P:T]
                return e.affine_select(out=tri, in_=tri, compare_op=ALU.is_ge, fill=NEG,
                                       base=0, pattern=[[-1, P]], channel_multiplier=1)
            add("pool", "masks", shapes)

            def ones(e):
                e.iota(iota_e[:], pattern=[[1, NE]], base=0, channel_multiplier=0,
                       allow_small_or_imprecise_dtypes=True)
                for r in range(2):
                    last = e.memset(vp[:, r, :, :, PARTS:VS], 1.0)
                return last
            add("pool", "ones_v", ones)

            def ones_k(e):
                need(e, "ones_v")
                return e.memset(f32(k_st[MAXROW:ROWS, :, :]), 1.0)
            add("pool", "ones", ones_k)

            def after_ones(e):
                need(e, "ones")
                return e.memset(half_neg, -0.5)
            add("pool", "consts", after_ones)

        def load_batch(b, what):
            r = b % 2

            def tile_of_x(t):
                def go(e, s):
                    e.dma_start(xc[:, r, t, :], x[b, t * P:(t + 1) * P, :]).then_inc(s, 16)
                return go

            def load_ctx(e, s):
                if b >= 2:
                    need(e, ("v3", b - 2), ("rope_w", b - 2, 0))
                e.dma_start(ct[:, r], ctx_in[b].rearrange("(t p) n -> p t n", p=P)).then_inc(s, 16)

            def load_x(e, s):
                if b >= 2:
                    need(e, ("x1", (b - 2) * TT + TT - 1))
                e.dma_start(xc[:, r], x[b].rearrange("(t p) n -> p t n", p=P)).then_inc(s, 16)

            if what == "ctx":
                plan.load(("ctx", b), f"c_b{r}", 1, load_ctx)
            elif b == 0:
                for t in range(TT):
                    plan.load(("x", b, t), f"x{t}", 1, tile_of_x(t))
            else:
                stream = "x_b1" if r else "x0"
                plan.load(("x", b, 0), stream, 1, load_x)
                for t in range(1, TT):
                    plan.reached[("x", b, t)] = plan.reached[("x", b, 0)]

        def load_constants(e, s):
            e.dma_start(cos_t[:], rope_cos.rearrange("(t p) d -> p t d", p=P)).then_inc(s, 16)
            e.dma_start(sin_t[:], rope_sin.rearrange("(t p) d -> p t d", p=P)).then_inc(s, 16)
            e.dma_start(wk_b[:], k_norm_w.partition_broadcast(P)).then_inc(s, 16)
            e.dma_start(wq_b[:], q_norm_w.partition_broadcast(P)).then_inc(s, 16)

        def key_scale(b):
            r = b % 2
            for t in range(TT):
                def ssq(e, t=t):
                    need(e, ("ctx", b))
                    if b >= 2:
                        need(e, ("k_eps", b - 2))
                    if b >= 1:
                        need(e, ("ssq", b - 1, t))
                    return e.tensor_tensor_reduce(junk[:, t, :], ct[:, r, t, :], ct[:, r, t, :],
                                                  1.0 / KVW, 0.0, ALU.mult, ALU.add, ssk[:, r, t:t + 1])
                add("dve", ("ssq", b, t), ssq)
            k_eps, r_k = sc[:, r, 1, :], sc[:, r, 3, :]

            def eps(e):
                need(e, ("ssq", b, TT - 1), "consts")
                if b >= 2:
                    need(e, ("k_tables", b - 2))
                return e.tensor_scalar(k_eps, ssk[:, r, :], EPS, None, ALU.add)
            add("pool", ("k_eps", b), eps)

            def power(e):
                need(e, ("k_eps", b))
                return e.tensor_tensor(r_k, k_eps, half_neg[:, 0:TT], ALU.pow)
            add("pool", ("k_pow", b), power)
            scaled_tables(b, "k", 1, r_k, ("k_pow", b), ("rope", b - 2, 0))

        def query_scale(b):
            r = b % 2
            for t in range(TT):
                def bn(e, t=t):
                    need(e, ("x", b, t))
                    return e.bn_stats(stats[:, r, t, :], xc[:, r, t, :])
                add("dve", ("bn", b, t), bn)
            for t in range(TT):
                def agg(e, t=t):
                    need(e, ("bn", b, t))
                    if b >= 2 and t == 0:
                        need(e, ("eps2", b - 2))
                    return e.bn_aggr(mv[:, r, t, :], stats[:, r, t, :])
                add("dve", ("agg", b, t), agg)
            for t in range(TT):
                def center(e, t=t):
                    need(e, ("agg", b, t))
                    return e.tensor_scalar(xc[:, r, t, :], xc[:, r, t, :], mv[:, r, t, 0:1], None,
                                           ALU.subtract)
                add("dve", ("center", b, t), center)
            var = mv[:, r, :, 1]
            v_eps, r_ln, v1, v2, s_rms, s_q = (sc[:, r, i, :] for i in (0, 2, 4, 5, 6, 7))

            def eps1(e):
                need(e, ("agg", b, TT - 1), "consts")
                if b >= 2:
                    need(e, ("q_tables", b - 2))
                return e.tensor_scalar(v_eps, var, EPS, None, ALU.add)
            add("pool", ("eps1", b), eps1)

            def pow_a(e):
                need(e, ("eps1", b), "consts")
                return e.tensor_tensor(r_ln, v_eps, half_neg[:, 0:TT], ALU.pow)
            add("pool", ("pow_b", b), pow_a)

            def sq1(e):
                need(e, ("pow_b", b))
                return e.tensor_tensor(v1, var, r_ln, ALU.mult)
            add("pool", ("sq1", b), sq1)

            def sq2(e):
                need(e, ("sq1", b))
                return e.tensor_tensor(v2, v1, r_ln, ALU.mult)
            add("pool", ("sq2", b), sq2)

            def eps2(e):
                need(e, ("sq2", b))
                return e.tensor_scalar(v1, v2, EPS, None, ALU.add)
            add("pool", ("eps2", b), eps2)

            def pow_q(e):
                need(e, ("eps2", b))
                return e.tensor_tensor(s_rms, v1, half_neg[:, 0:TT], ALU.pow)
            add("pool", ("pow_q", b), pow_q)

            def scale_q(e):
                need(e, ("pow_q", b))
                return e.tensor_tensor(s_q, s_rms, r_ln, ALU.mult)
            add("pool", ("scale_q", b), scale_q)

            scaled_tables(b, "q", 0, s_q, ("scale_q", b), ("rope", b - 2, KV))

        def scaled_tables(b, name, i, scale, ready, last_use):
            def tables(e):
                need(e, ready, "tables_in")
                if b >= 2:
                    need(e, last_use)
                for j, tab in enumerate((cos_t, sin_t)):
                    last = e.tensor_tensor(csq[:, b % 2, i, j], tab[:],
                                           scale.unsqueeze(2).broadcast_to([P, TT, D]), ALU.mult)
                return last
            add("pool", (name + "_tables", b), tables)

        def rope(b, i):
            r, n = b % 2, b * (KV + 1) + i
            q = n % 2
            src = ct[:, r] if i == 0 else xc[:, r, :, (i - 1) * P:i * P]
            w = wk_b[:] if i == 0 else wq_b[:, (i - 1) * P:i * P]
            cs, sn = csq[:, r, 1 if i == 0 else 0, 0], csq[:, r, 1 if i == 0 else 0, 1]
            wb = w.unsqueeze(1).broadcast_to([P, TT, P])
            heads = lambda ap: ap.rearrange("p t (h d) -> p t h d", d=D)
            prev = n - 2
            pb, pi = prev // (KV + 1), prev % (KV + 1)
            lb, li = (n - 1) // (KV + 1), (n - 1) % (KV + 1)

            def weigh(e):
                if i == 0:
                    need(e, ("ctx", b), "tables_in")
                else:
                    need(e, ("center", b, TT - 1), "tables_in")
                if prev >= 0:
                    need(e, ("rope", pb, pi))
                return e.tensor_tensor(rw_b[:, q], src, wb, ALU.mult)
            add("pool", ("rope_w", b, i), weigh)

            def cosine(e):
                need(e, ("rope_w", b, i), ("k_tables" if i == 0 else "q_tables", b))
                if prev >= 0:
                    need(e, ("turn", pb, pi))
                return e.tensor_tensor(heads(r1_b[:, q]), heads(rw_b[:, q]),
                                       cs.unsqueeze(2).broadcast_to([P, TT, P // D, D]), ALU.mult)
            add("dve", ("rope_c", b, i), cosine)

            def sine(e):
                need(e, ("rope_w", b, i), ("k_tables" if i == 0 else "q_tables", b))
                if n >= 1:
                    need(e, ("rope", lb, li))
                for lo, hi in ((0, HALF), (HALF, 0)):
                    last = e.tensor_tensor(
                        heads(r2_b[:])[:, :, :, lo:lo + HALF], heads(rw_b[:, q])[:, :, :, hi:hi + HALF],
                        sn[:, :, lo:lo + HALF].unsqueeze(2).broadcast_to([P, TT, P // D, HALF]), ALU.mult)
                return last
            add("pool", ("rope_s", b, i), sine)

            def total(e):
                need(e, ("rope_c", b, i), ("rope_s", b, i))
                return e.tensor_tensor(r1_b[:, q], r1_b[:, q], r2_b[:], ALU.add)
            add("dve", ("rope", b, i), total)

        m_items = []

        def take_m_bank(reader):
            m_items.append(reader)
            n = len(m_items) - 1
            return m_bank[n % 2], (m_items[n - 2] if n >= 2 else None)

        def turn_in(b, i):
            n = b * (KV + 1) + i
            q = n % 2
            dst, before = take_m_bank(("turned_l", b, i))

            def turn(e):
                need(e, ("rope", b, i), "masks")
                if before:
                    need(e, before)
                for t in range(TT):
                    last = e.transpose(dst[:, t * P:(t + 1) * P], r1_b[:, q, t, :], ident[:])
                return last
            add("pe", ("turn", b, i), turn)

            def split_h(e):
                need(e, ("turn", b, i))
                if n >= 2:
                    need(e, ("stacked", n - 2))
                return e.activation(turned_h[:, q, :], dst[:], ACT.Copy)
            add("act", ("turned_h", b, i), split_h)

            def split_l(e):
                need(e, ("turned_h", b, i))
                if n >= 2:
                    need(e, ("stacked", n - 2))
                return e.tensor_tensor(turned_l[:, q, :], dst[:], f32(turned_h[:, q, :]), ALU.subtract)
            add("dve", ("turned_l", b, i), split_l)

            if i == 0:
                for j in range(KV):
                    c = b * KV + j

                    def stack_k(e, s, j=j, c=c):
                        need(e, ("turned_l", b, i))
                        if c >= KR:
                            need(e, ("pass_b", (c - KR) * G + G - 1))
                        for row, part in ((0, turned_h), (D, turned_l), (2 * D, turned_h)):
                            e.dma_start(f32(k_st[row:row + D, c % KR, :]),
                                        f32(part[j * D:(j + 1) * D, q, :])).then_inc(s, 16)
                    plan.load(("k_st", c), f"k{c % KR}", 3, stack_k)
            else:
                c = b * KV + i - 1

                def stack_q(e, s):
                    need(e, ("turned_l", b, i))
                    if c >= QR:
                        need(e, ("pass_b", (c - QR) * G + G - 1))
                    for j in range(G):
                        for row, part in ((0, turned_h), (D, turned_h), (2 * D, turned_l)):
                            e.dma_start(f32(q_st[row:row + D, c % QR, j, :]),
                                        f32(part[j * D:(j + 1) * D, q, :])).then_inc(s, 16)
                plan.load(("q_st", c), f"q{c % QR}", 3 * G, stack_q)
            stacked = [("k_st", b * KV + j) for j in range(KV)] if i == 0 else [("q_st", b * KV + i - 1)]
            aliases[("stacked", n)] = stacked

        def values(b):
            r = b % 2
            part = lambda k: vp[:, r, :, :, k * D:(k + 1) * D]
            heads = lambda ap: ap.rearrange("p t (h d) -> p t h d", d=D)

            def v1(e):
                need(e, ("ctx", b))
                if b >= 2:
                    need(e, ("pv", (b - 1) * KV * G - 1))
                return e.tensor_copy(part(0), heads(ct[:, r]))
            add("dve", ("v1", b), v1)

            def rest(e):
                need(e, ("v1", b))
                return e.tensor_tensor(heads(vr[:]), heads(ct[:, r]), part(0), ALU.subtract)
            add("dve", ("vr", b), rest)

            def v2(e):
                need(e, ("vr", b))
                return e.tensor_copy(part(1), heads(vr[:]))
            add("dve", ("v2", b), v2)

            def v3(e):
                need(e, ("v2", b))
                return e.tensor_tensor(part(2), heads(vr[:]), part(1), ALU.subtract)
            add("dve", ("v3", b), v3)

        def pass_a(n):
            c, j = n // G, n % G
            for t in range(TT):
                i = n * TT + t
                s = a_bank[i % 2]
                width = (t + 1) * P

                def scores(e, t=t, i=i, s=s, width=width):
                    need(e, ("k_st", c), ("q_st", c))
                    if i >= 2:
                        need(e, ("max", (i - 2) // TT, (i - 2) % TT))
                    w = max(width, 2 * P)
                    return e.matmul(s[:, 0:w], q_st[0:MAXROW, c % QR, j, t * P:(t + 1) * P],
                                    k_st[0:MAXROW, c % KR, 0:w], start=True, stop=True)
                add("pe", ("pass_a", n, t), scores)

                def row_max(e, t=t, s=s, width=width):
                    need(e, ("pass_a", n, t), "masks")
                    if c >= 2 and j == 0 and t == 0:
                        need(e, ("m_lo", c - 2))
                    return e.tensor_tensor_reduce(s[:, 0:width], s[:, 0:width],
                                                  mask_qk[:, T - width:T], 1.0, -3e38, ALU.add, ALU.max,
                                                  mx[:, c % 2, t, j:j + 1])
                add("dve", ("max", n, t), row_max)

        def maxima(c):
            r = c % 2
            hi, lo = mhl[:, r, :, 0:G], mhl[:, r, :, G:2 * G]
            dst, before = take_m_bank(("m_t", c))

            def m_hi(e):
                need(e, ("max", c * G + G - 1, TT - 1))
                if c >= 2:
                    need(e, ("m_turn", c - 2))
                return e.tensor_scalar(hi, mx[:, r], -1.0, None, ALU.mult)
            add("dve", ("m_hi", c), m_hi)

            def m_lo(e):
                need(e, ("m_hi", c))
                return e.scalar_tensor_tensor(lo, mx[:, r], -1.0, f32(hi), ALU.mult, ALU.subtract)
            add("dve", ("m_lo", c), m_lo)

            def m_turn(e):
                need(e, ("m_lo", c), "masks")
                if before:
                    need(e, before)
                for t in range(TT):
                    last = e.transpose(dst[0:2 * G, t * P:(t + 1) * P], f32(mhl[:, r, t, :]), ident[:])
                return last
            add("pe", ("m_turn", c), m_turn)

            def m_out(e):
                need(e, ("m_turn", c))
                if c >= 1:
                    need(e, ("m_rows", c - 1))
                return e.activation(m_t[:], dst[0:2 * G, :], ACT.Copy)
            add("act", ("m_t", c), m_out)

            def rows(e, s):
                need(e, ("m_t", c))
                if c >= QR:
                    need(e, ("pass_b", (c - QR) * G + G - 1))
                for k in range(2):
                    e.dma_start(f32(q_st[MAXROW + k:MAXROW + k + 1, c % QR, :, :]),
                                f32(m_t[k * G:(k + 1) * G, :])).then_inc(s, 16)
            plan.load(("m_rows", c), f"m{r}", 2, rows)

        def pass_b(n):
            c, j, r = n // G, n % G, n % 2

            def tile_scores(e, k, out_ap, q0, mask_at):
                e.matmul(out_ap, k_st[:, c % KR, k * P:(k + 1) * P], q_st[:, c % QR, j, q0:T],
                         start=True, stop=True)
                return e.matmul(mask_at, ident16[:], mask_kq[:], start=False, stop=True,
                                skip_group_check=True)

            def scores_x(e):
                need(e, ("m_rows", c), "masks", "ones")
                if n >= 1:
                    need(e, ("exp_x16", n - 1))
                for k in range(2):
                    last = tile_scores(e, k, pair[:, BASE[k]:BASE[k] + T - k * P], k * P,
                                       pair[:, BASE[k]:BASE[k] + P])
                return last
            add("pe", ("pass_bx", n), scores_x)

            def scores_y(e):
                if n >= 1:
                    need(e, ("exp_y16", n - 1))
                tile_scores(e, 3, b_bank[:, P:3 * P], 2 * P, b_bank[:, 2 * P:3 * P])
                return tile_scores(e, 2, b_bank[:, 0:2 * P], 2 * P, b_bank[:, 0:P])
            add("pe", ("pass_b", n), scores_y)

            for name, src, at, width in (("x", pair, 0, XW), ("y", b_bank, XW, YW)):
                def exp32(e, name=name, src=src, at=at, width=width):
                    need(e, ("pass_bx" if name == "x" else "pass_b", n), "zeroed")
                    if n >= 2:
                        need(e, (f"p_l{name}", n - 2))
                    return e.activation(p32[:, r, at:at + width], src[:, 0:width], ACT.Exp,
                                        bias=log256, scale=SCALE)
                add("act", (f"exp_{name}32", n), exp32)

                def exp16(e, name=name, src=src, at=at, width=width):
                    if n >= 2:
                        need(e, ("pv", n - 2))
                    return e.activation(p_h[:, r, at:at + width], src[:, 0:width], ACT.Exp,
                                        bias=log256, scale=SCALE)
                add("act", (f"exp_{name}16", n), exp16)

                def low(e, name=name, at=at, width=width):
                    need(e, (f"exp_{name}16", n))
                    if n >= 2:
                        need(e, ("pv", n - 2))
                    return e.tensor_tensor(p_l[:, r, at:at + width], p32[:, r, at:at + width],
                                           p_h[:, r, at:at + width], ALU.subtract)
                add("dve", (f"p_l{name}", n), low)

        def value_product(n):
            c, j, r = n // G, n % G, n % 2
            b, kv = c // KV, c % KV

            def pv(e):
                need(e, ("p_ly", n), ("v3", b))
                if n >= 1:
                    need(e, ("osb", n - 1))
                for t in range(TT):
                    for k in range(t + 1):
                        for m, p in enumerate((p_h, p_l)):
                            at = BASE[k] + (t - k) * P
                            last = e.matmul(v_bank[:, t * VS:t * VS + VS - 1], p[:, r, at:at + P],
                                            vp[:, b % 2, k, kv, 0:VS - 1],
                                            start=(k == 0 and m == 0), stop=(k == t and m == 1))
                return last
            add("pe", ("pv", n), pv)

            def evacuate(e):
                need(e, ("pv", n))
                if c >= 2 and j == 0:
                    need(e, ("norm", c - 2))
                src = v_bank[:, 0:TT * VS].rearrange("p (t v) -> p t v", v=VS)[:, :, 0:VS - 1]
                return e.activation(osb[:, c % 2, j, :, 0:VS - 1], src, ACT.Copy)
            add("act", ("osb", n), evacuate)

        def combine(c):
            r, kv = c % 2, c % KV
            b = c // KV
            part = lambda k: osb[:, r, :, :, k * D:(k + 1) * D]
            dst = att[:].rearrange("p t (h d) -> p h t d", d=D)

            def inverse(e):
                need(e, ("osb", c * G + G - 1))
                if c >= 2:
                    need(e, ("norm", c - 2))
                return e.reciprocal(rinv[:, r], osb[:, r, :, :, PARTS])
            add("dve", ("rinv", c), inverse)

            def add12(e):
                need(e, ("osb", c * G + G - 1))
                return e.tensor_tensor(part(0), part(0), part(1), ALU.add)
            add("pool", ("add12", c), add12)

            def add3(e):
                need(e, ("add12", c))
                return e.tensor_tensor(part(0), part(0), part(2), ALU.add)
            add("pool", ("add3", c), add3)

            def norm(e):
                need(e, ("add3", c), ("rinv", c))
                if c >= 1:
                    need(e, ("o_turn", c - 1))
                return e.tensor_tensor(dst, part(0), rinv[:, r].unsqueeze(3).broadcast_to([P, G, TT, D]),
                                       ALU.mult)
            add("pool", ("norm", c), norm)

        def turn_out(c):
            r, kv, b = c % 2, c % KV, c // KV
            dst_m, before = take_m_bank(("o_l", c))

            def turn(e):
                need(e, ("norm", c), before)
                for t in range(TT):
                    last = e.transpose(dst_m[:, t * P:(t + 1) * P], att[:, t, :], ident[:])
                return last
            add("pe", ("o_turn", c), turn)

            def split_h(e):
                need(e, ("o_turn", c))
                if b >= 1:
                    need(e, ("proj", b * TT - 1))
                return e.activation(o_h[:, kv, :], dst_m[:], ACT.Copy)
            add("act", ("o_h", c), split_h)

            def split_l(e):
                need(e, ("o_h", c))
                if b >= 1:
                    need(e, ("proj", b * TT - 1))
                return e.tensor_tensor(o_l[:, kv, :], dst_m[:], f32(o_h[:, kv, :]), ALU.subtract)
            add("dve", ("o_l", c), split_l)

        def project(g):
            b, t = g // TT, g % TT
            dst, before = take_m_bank(("x1", g))

            def proj(e):
                need(e, ("o_l", b * KV + KV - 1), before, ("wo_l", KC - 1))
                for k in range(KC):
                    rows = slice(t * P, (t + 1) * P)
                    for m, (o, w) in enumerate(((o_h, wo_h), (o_h, wo_l), (o_l, wo_h))):
                        last = e.matmul(dst[:], o[:, k, rows], w[:, k, :], start=(k == 0 and m == 0),
                                        stop=(k == KC - 1 and m == 2))
                return last
            add("pe", ("proj", g), proj)

            def residual(e):
                need(e, ("proj", g))
                return e.scalar_tensor_tensor(x1[:, g, :], dst[:], mv[:, b % 2, t, 0:1],
                                              xc[:, b % 2, t, :], ALU.add, ALU.add)
            add("dve", ("x1", g), residual)

        def output_weights():
            def load(e, s):
                e.dma_start(raw[:], w_out.rearrange("(t p) n -> p t n", p=P)).then_inc(s, 16)
            plan.load("wo_raw", "wo", 1, load)
            for k in range(KC):
                dst, before = take_m_bank(("wo_l", k))

                def turn(e, k=k, dst=dst, before=before):
                    need(e, "wo_raw", "masks")
                    if before:
                        need(e, before)
                    for t in range(KC):
                        last = e.transpose(dst[:, t * P:(t + 1) * P], raw[:, t, k * P:(k + 1) * P],
                                           ident[:])
                    return last
                add("pe", ("wo_turn", k), turn)

                def split_h(e, k=k, dst=dst):
                    need(e, ("wo_turn", k))
                    return e.activation(wo_h[:, k, :], dst[:], ACT.Copy)
                add("act", ("wo_h", k), split_h)

                def split_l(e, k=k, dst=dst):
                    need(e, ("wo_h", k))
                    return e.tensor_tensor(wo_l[:, k, :], dst[:], f32(wo_h[:, k, :]), ALU.subtract)
                add("dve", ("wo_l", k), split_l)

        def mixture_table():
            def load(e, s):
                e.dma_start(amp[:], amplitudes).then_inc(s, 16)
                e.dma_start(es[:, 0:1], expert_scale.rearrange("(e o) -> e o", o=1)).then_inc(s, 16)
            plan.load("amps", "amps", 2, load)

            def square(e):
                need(e, "amps")
                return e.tensor_tensor(amp[:], amp[:], amp[:], ALU.mult)
            add("dve", "amp_sq", square)

            def power(e):
                need(e, "amp_sq")
                return e.tensor_tensor(amp_s[:], amp[:, :, 0], amp[:, :, 1], ALU.add)
            add("dve", "amp_s", power)

            def total(e):
                need(e, "amp_s")
                return e.tensor_reduce(es[:, 1:2], amp_s[:], AX.X, ALU.add)
            add("dve", "amp_sum", total)

            def eps(e):
                need(e, "amp_sum")
                return e.tensor_scalar(es[:, 2:3], es[:, 1:2], EPS_FFN, None, ALU.add)
            add("dve", "amp_eps", eps)

            def inverse(e):
                need(e, "amp_eps")
                return e.reciprocal(es[:, 3:4], es[:, 2:3])
            add("dve", "amp_inv", inverse)

            def scaled(e):
                need(e, "amp_inv")
                return e.tensor_scalar(mixs[:], amp_s[:], es[:, 3:4], es[:, 0:1], ALU.mult, ALU.mult)
            add("dve", "mixs", scaled)

        attention_over = [("x1", NT - 1), ("proj", NT - 1), ("p_ly", NH - 1), ("norm", NC - 1),
                          ("osb", NH - 1), ("m_rows", NC - 1)]

        raw_uses = []

        def split_weights(name, source, dst_h, dst_l, slots, ready):
            for h in range(0, slots, 2):
                n = len(raw_uses)
                side = n % 2
                src = raw[:, 2 * side:2 * side + min(2, slots - h), :]

                def load(e, s, h=h, n=n, src=src):
                    need(e, ("wo_turn", KC - 1))
                    if n >= 2:
                        need(e, raw_uses[n - 2])
                    for dst, part in source(h, src):
                        e.dma_start(dst, part).then_inc(s, 16)
                plan.load((name, "raw", h), f"raw{side}", len(source(h, src)), load)
                for k in range(h, min(h + 2, slots)):
                    def split_h(e, k=k, h=h, src=src):
                        need(e, (name, "raw", h), *ready)
                        return e.activation(dst_h(k), src[:, k - h, :], ACT.Copy)
                    add("act", (name, "h", k), split_h)

                    def split_l(e, k=k, h=h, src=src):
                        need(e, (name, "h", k), *ready)
                        return e.tensor_tensor(dst_l(k), src[:, k - h, :], f32(dst_h(k)), ALU.subtract)
                    add("dve", (name, "l", k), split_l)
                raw_uses.append((name, "l", min(h + 1, slots - 1)))

        def chunk_weights(w):
            gate, up, at = (w_gate, w_up, w * I) if w < NK else (shared_w_gate, shared_w_up, (w - NK) * I)

            def source(h, dst):
                view = lambda m: m[h * P:(h + 2) * P, at:at + I].rearrange("(k p) n -> p k n", p=P)
                return [(dst[:, :, 0:I], view(gate)), (dst[:, :, I:2 * I], view(up))]
            ready = [("unit", w - 2, NT - 1)] if w >= 2 else attention_over
            split_weights(("w", w), source, lambda k: w_h[:, w % 2, k, :], lambda k: w_l[:, w % 2, k, :],
                          KC, ready)

        def router_weights():
            n = len(raw_uses)
            side = n % 2
            src = raw[:, 2 * side, :].rearrange("p (k n) -> p k n", n=NE)

            def load(e, s):
                if n >= 2:
                    need(e, raw_uses[n - 2])
                need(e, ("wo_turn", KC - 1))
                e.dma_start(src, w_router.rearrange("(k p) n -> p k n", p=P)).then_inc(s, 16)
            plan.load("rt_raw", f"raw{side}", 1, load)

            def split_h(e):
                need(e, "rt_raw", *attention_over)
                return e.activation(rt_w[:, :, 0:NE], src, ACT.Copy)
            add("act", "rt_h", split_h)

            def split_l(e):
                need(e, "rt_h")
                return e.tensor_tensor(rt_w[:, :, NE:2 * NE], src, f32(rt_w[:, :, 0:NE]), ALU.subtract)
            add("dve", "rt_l", split_l)
            raw_uses.append("rt_l")

        def down_weights():
            def source_of(m):
                return lambda h, dst: [(dst, m[h * P:(h + 2) * P, :].rearrange("(k p) n -> p k n", p=P))]
            split_weights("wd", source_of(w_down), lambda k: wd_h[:, k, :], lambda k: wd_l[:, k, :],
                          I // P, attention_over)
            split_weights("ws", source_of(shared_w_down), lambda k: ws_h[:, k, :],
                          lambda k: ws_l[:, k, :], NS * I // P, [("wt", NT - 1), ("cf_t", NT - 1)])

        f_items, y_items, g_items = [], [], []

        def take(items, banks, reader):
            items.append(reader)
            n = len(items) - 1
            return banks[n % len(banks)], (items[n - len(banks)] if n >= len(banks) else None)

        def normalize(g):
            r = g % 2

            def bn(e):
                need(e, ("x1", g), *attention_over)
                return e.bn_stats(st2[:, r, :], x1[:, g, :])
            add("dve", ("bn2", g), bn)

            def agg(e):
                need(e, ("bn2", g))
                if g >= 2:
                    need(e, ("eps3", g - 2))
                return e.bn_aggr(mv2[:, r, :], st2[:, r, :])
            add("dve", ("agg2", g), agg)

            def eps(e):
                need(e, ("agg2", g))
                return e.tensor_scalar(s2[:, r, 0:1], mv2[:, r, 1:2], EPS, None, ALU.add)
            add("pool", ("eps3", g), eps)

            def power(e):
                need(e, ("eps3", g))
                if g >= 2:
                    need(e, ("xn", g - 2))
                return e.tensor_tensor(s2[:, r, 1:2], s2[:, r, 0:1], half_neg[:, 0:1], ALU.pow)
            add("pool", ("rstd", g), power)

            def norm(e):
                need(e, ("rstd", g), ("agg2", g))
                if g >= 2:
                    need(e, ("x_turn", g - 2))
                return e.tensor_scalar(xn[:, r, :], x1[:, g, :], mv2[:, r, 0:1], s2[:, r, 1:2],
                                       ALU.subtract, ALU.mult)
            add("dve", ("xn", g), norm)

        def turn_x(g):
            r = g % 2
            dst, before = take(f_items, f_bank, ("t_l", g))
            view = dst[:].rearrange("p (k n) -> p k n", n=P)
            cols = slice(g * P, (g + 1) * P)

            def turn(e):
                need(e, ("xn", g))
                if before:
                    need(e, before)
                for k in range(KC):
                    last = e.transpose(view[:, k, :], xn[:, r, k * P:(k + 1) * P], ident[:])
                return last
            add("pe", ("x_turn", g), turn)

            def split_h(e):
                need(e, ("x_turn", g))
                return e.activation(t_h[:, :, cols], view, ACT.Copy)
            add("act", ("t_h", g), split_h)

            def split_l(e):
                need(e, ("t_h", g))
                return e.tensor_tensor(t_l[:, :, cols], view, f32(t_h[:, :, cols]), ALU.subtract)
            add("dve", ("t_l", g), split_l)

        def route(g):
            r = g % 2
            dst, before = take(y_items, y_bank, ("logits", g))
            cols = slice(g * P, (g + 1) * P)

            def logits_mm(e):
                need(e, ("t_l", g), "rt_l")
                if before:
                    need(e, before)
                for k in range(KC):
                    for m, t in enumerate((t_h, t_l)):
                        last = e.matmul(dst[:, 0:2 * NE], t[:, k, cols], rt_w[:, k, :],
                                        start=(k == 0 and m == 0), stop=(k == KC - 1 and m == 1))
                return last
            add("pe", ("route", g), logits_mm)

            def low_half(e):
                need(e, ("route", g))
                if g >= 2:
                    need(e, ("logits", g - 2))
                return e.activation(ex[:, r, :], dst[:, NE:2 * NE], ACT.Copy)
            add("act", ("lg_l", g), low_half)

            def logits(e):
                need(e, ("lg_l", g))
                return e.tensor_tensor(lg[:, r, :], dst[:, 0:NE], ex[:, r, :], ALU.add)
            add("dve", ("logits", g), logits)

            def neg_max(e):
                need(e, ("logits", g))
                return e.tensor_reduce(sm[:, r, 0:1], lg[:, r, :], AX.X, ALU.max, negate=True)
            add("dve", ("neg_max", g), neg_max)

            def expo(e):
                need(e, ("neg_max", g))
                return e.activation(ex[:, r, :], lg[:, r, :], ACT.Exp, bias=sm[:, r, 0:1],
                                    accum_out=sm[:, r, 1:2])
            add("act", ("router_exp", g), expo)

            def inv(e):
                need(e, ("router_exp", g))
                return e.reciprocal(sm[:, r, 2:3], sm[:, r, 1:2])
            add("dve", ("rsum", g), inv)

            def probs(e):
                need(e, ("rsum", g))
                return e.tensor_scalar(lg[:, r, :], ex[:, r, :], sm[:, r, 2:3], None, ALU.mult)
            add("dve", ("probs", g), probs)

            def largest(e):
                need(e, ("probs", g))
                return e.max(top[:, r, :], lg[:, r, :])
            add("dve", ("top", g), largest)

            def where(e):
                need(e, ("top", g))
                return e.max_index(idx[:, r, :], top[:, r, :], lg[:, r, :])
            add("dve", ("idx", g), where)

            def top_sum(e):
                need(e, ("top", g))
                return e.tensor_reduce(sm[:, r, 3:4], top[:, r, 0:TOPK], AX.X, ALU.add)
            add("dve", ("top_sum", g), top_sum)

            def as_float(e):
                need(e, ("idx", g))
                return e.tensor_copy(idf[:, r, :], idx[:, r, :])
            add("dve", ("idf", g), as_float)

            def top_eps(e):
                need(e, ("top_sum", g))
                return e.tensor_scalar(sm[:, r, 4:5], sm[:, r, 3:4], EPS_FFN, None, ALU.add)
            add("dve", ("top_eps", g), top_eps)

            def chosen(e):
                need(e, ("idf", g), "ones")
                if g >= 2:
                    need(e, ("cf_turn", g - 2))
                return e.tensor_scalar(cf[:, r, :], iota_e[:], idf[:, r, 0:1], None, ALU.is_equal)
            add("dve", ("chosen", g, 0), chosen)
            for k in range(1, TOPK):
                def more(e, k=k):
                    need(e, ("chosen", g, k - 1))
                    return e.scalar_tensor_tensor(cf[:, r, :], iota_e[:], idf[:, r, k:k + 1], cf[:, r, :],
                                                  ALU.is_equal, ALU.add)
                add("dve", ("chosen", g, k), more)

            def top_inv(e):
                need(e, ("top_eps", g))
                if g >= 2:
                    need(e, ("wt", g - 2))
                return e.reciprocal(sm[:, r, 5:6], sm[:, r, 4:5])
            add("dve", ("top_inv", g), top_inv)

            def half(e):
                need(e, ("top_inv", g))
                return e.tensor_scalar(sm[:, r, 6:7], sm[:, r, 5:6], 0.5, None, ALU.mult)
            add("dve", ("half_inv", g), half)

            def coeff(e):
                need(e, ("chosen", g, TOPK - 1), ("probs", g))
                return e.tensor_tensor(cf[:, r, :], cf[:, r, :], lg[:, r, :], ALU.mult)
            add("dve", ("coeff", g), coeff)

        def mix_weights(g):
            r = g % 2
            dst, before = take(f_items, f_bank, ("cf_t", g))

            def turn(e):
                need(e, ("coeff", g))
                if before:
                    need(e, before)
                return e.transpose(dst[:, 0:P], cf[:, r, :], ident[:])
            add("pe", ("cf_turn", g), turn)

            def evacuate(e):
                need(e, ("cf_turn", g))
                if g >= 2:
                    need(e, ("mix", g - 2))
                return e.activation(cf_t[:, r, :], dst[:, 0:P], ACT.Copy)
            add("act", ("cf_t", g), evacuate)

            dst2, before2 = take(y_items, y_bank, ("wt", g))

            def mix(e):
                need(e, ("cf_t", g), "mixs")
                if before2:
                    need(e, before2)
                return e.matmul(dst2[:, 0:NK], cf_t[:, r, :], mixs[:], start=True, stop=True)
            add("pe", ("mix", g), mix)

            def scaled(e):
                need(e, ("mix", g), ("half_inv", g))
                return e.tensor_scalar(wt[:, g, :], dst2[:, 0:NK], sm[:, r, 6:7], None, ALU.mult)
            add("dve", ("wt", g), scaled)

        def unit(w, g):
            n = len(g_items)
            r = n % 2
            dst, before = take(g_items, g_bank, ("gb", w, g))
            cols = slice(g * P, (g + 1) * P)
            gate, up = dst[:, 0:I], dst[:, I:2 * I]
            shared = w >= NK

            def mm(e):
                need(e, ("t_l", g), (("w", w), "l", KC - 1))
                if before:
                    need(e, before)
                for k in range(KC):
                    for m, (t, ww) in enumerate(((t_h, w_h), (t_h, w_l), (t_l, w_h))):
                        last = e.matmul(dst[:, 0:2 * I], t[:, k, cols], ww[:, w % 2, k, :],
                                        start=(k == 0 and m == 0), stop=(k == KC - 1 and m == 2))
                return last
            add("pe", ("unit", w, g), mm)
            two_before = g_items[n - 2] if n >= 2 else None

            def tanh(e):
                need(e, ("unit", w, g))
                if n >= 2:
                    need(e, ("ga",) + g_items[n - 2][1:])
                return e.activation(th[:, r, :], gate, ACT.Tanh, scale=0.5)
            add("act", ("th", w, g), tanh)

            def first(e):
                need(e, ("th", w, g))
                return e.scalar_tensor_tensor(ga[:, r, :], th[:, r, :], 1.0, up, ALU.add, ALU.mult)
            add("dve", ("ga", w, g), first)

            if shared:
                to = hs[:, g % 2, (w - NK) * I:(w - NK + 1) * I]
            elif w == 0:
                to = macc[:, g, :]
            else:
                to = gb[:, r, :]

            def second(e):
                need(e, ("ga", w, g))
                if shared:
                    if g >= 2:
                        need(e, ("d_turn", g - 2))
                    scale = 0.5
                else:
                    need(e, ("wt", g))
                    scale = wt[:, g, w:w + 1]
                    if w > 0 and two_before and two_before[1] > 0:
                        need(e, ("acc",) + two_before[1:])
                return e.scalar_tensor_tensor(to, ga[:, r, :], scale, gate, ALU.mult, ALU.mult)
            add("dve", ("gb", w, g), second)

            if not shared and w > 0:
                def accumulate(e):
                    need(e, ("gb", w, g), ("gb", 0, g))
                    if w > 1:
                        need(e, ("acc", w - 1, g))
                    return e.tensor_tensor(macc[:, g, :], macc[:, g, :], gb[:, r, :], ALU.add)
                add("pool", ("acc", w, g), accumulate)

        def turn_down(g):
            r = g % 2
            blocks = [("m", k) for k in range(I // P)] + [("s", k) for k in range(NS * I // P)]
            for half in range(2):
                part = blocks[half * 3:half * 3 + 3]
                dst, before = take(f_items, f_bank, ("d_l", g, half))

                def turn(e, part=part, dst=dst, before=before):
                    need(e, ("gb", NW - 1, g), ("gb", NW - 2, g), ("acc", NK - 1, g))
                    if before:
                        need(e, before)
                    for i, (kind, k) in enumerate(part):
                        src = macc[:, g, k * P:(k + 1) * P] if kind == "m" else hs[:, r, k * P:(k + 1) * P]
                        last = e.transpose(dst[:, i * P:(i + 1) * P], src, ident[:])
                    return last
                name = ("d_turn", g) if half else ("d_turn0", g)
                add("pe", name, turn)
                view = dst[:, 0:3 * P].rearrange("p (k n) -> p k n", n=P)
                rows = slice(half * 3, half * 3 + 3)

                def split_h(e, name=name, view=view, rows=rows):
                    need(e, name)
                    if g >= 2:
                        need(e, ("down", g - 2))
                    return e.activation(d_h[:, r, rows, :], view, ACT.Copy)
                add("act", ("d_h", g, half), split_h)

                def split_l(e, half=half, view=view, rows=rows):
                    need(e, ("d_h", g, half))
                    if g >= 2:
                        need(e, ("down", g - 2))
                    return e.tensor_tensor(d_l[:, r, rows, :], view, f32(d_h[:, r, rows, :]), ALU.subtract)
                add("dve", ("d_l", g, half), split_l)

        def down(g):
            r = g % 2
            dst, before = take(y_items, y_bank, ("done", g))
            weights = ([(wd_h[:, k, :], wd_l[:, k, :]) for k in range(I // P)]
                       + [(ws_h[:, k, :], ws_l[:, k, :]) for k in range(NS * I // P)])

            def mm(e):
                need(e, ("d_l", g, 1), ("d_l", g, 0), ("wd", "l", I // P - 1),
                     ("ws", "l", NS * I // P - 1), before)
                for k, (wh, wl) in enumerate(weights):
                    for m, (dd, ww) in enumerate(((d_h, wh), (d_h, wl), (d_l, wh))):
                        last = e.matmul(dst[:], dd[:, r, k, :], ww, start=(k == 0 and m == 0),
                                        stop=(k == ND - 1 and m == 2))
                return last
            add("pe", ("down", g), mm)

            def finish(e):
                need(e, ("down", g))
                return e.tensor_tensor(x1[:, g, :], x1[:, g, :], dst[:], ALU.add)
            add("dve", ("done", g), finish)

            def store(e, s):
                need(e, ("done", g))
                b, t = g // TT, g % TT
                e.dma_start(out[b, t * P:(t + 1) * P, :], x1[:, g, :]).then_inc(s, 16)
            plan.load(("stored", g), f"out{g % 2}", 1, store)

        aliases = {}
        plain_need = plan.need

        def need_with_aliases(engine, *names):
            for name in names:
                for real in aliases.get(name, [name]):
                    plain_need(engine, real)
        need = need_with_aliases

        constants()
        load_batch(0, "ctx")
        load_batch(0, "x")
        plan.load("tables_in", "consts", 4, load_constants)
        output_weights()
        mixture_table()
        load_batch(1, "ctx")
        load_batch(1, "x")

        for n in range(-15, NH + 12):
            for b in range(B):
                first = b * KV * G
                if b >= 2 and n == first - 15:
                    load_batch(b, "ctx")
                if b >= 2 and n == first - 11:
                    load_batch(b, "x")
                if n == first - 14:
                    key_scale(b)
                if n == first - 13:
                    rope(b, 0)
                if n == first - 12:
                    turn_in(b, 0)
                    values(b)
                if n == first - 10:
                    query_scale(b)
            for c in range(NC):
                b, i = c // KV, c % KV + 1
                late = 1 if i == 1 else 0
                if n == c * G - 10 + late:
                    rope(b, i)
                if n == c * G - 9 + late:
                    turn_in(b, i)
            if 0 <= n + LEAD < NH:
                pass_a(n + LEAD)
            for c in range(NC):
                if n == c * G - 2:
                    maxima(c)
            if 0 <= n < NH:
                pass_b(n)
            if 0 <= n - 1 < NH:
                value_product(n - 1)
            for c in range(NC):
                if n == c * G + 4:
                    combine(c)
                if n == c * G + 6:
                    turn_out(c)
            for b in range(B):
                for t in range(TT):
                    if n == (b + 1) * KV * G + 3 + t // 2:
                        project(b * TT + t)

        chunk_weights(0)
        router_weights()
        for tick in range(-4, NT):
            if 0 <= tick + 4 < NT:
                normalize(tick + 4)
            if 0 <= tick + 3 < NT:
                turn_x(tick + 3)
            if 0 <= tick < NT:
                mix_weights(tick)
            if 0 <= tick + 2 < NT:
                route(tick + 2)
            if 0 <= tick < NT:
                unit(0, tick)
            if tick == 1:
                chunk_weights(1)
        for w in range(1, NK):
            for g in range(NT):
                unit(w, g)
                if g == 1:
                    chunk_weights(w + 1)
                if g == 8 and w == 1:
                    down_weights()
        chunk_weights(NK + 1)
        for g in range(NT + 1):
            if g < NT:
                for w in range(NK, NW):
                    unit(w, g)
                if g >= 1:
                    down(g - 1)
                turn_down(g)
            else:
                down(g - 1)

        def finish_all(e, s):
            need(e, ("stored", NT - 1), ("stored", NT - 2))
        plan.load("end", "out0", 0, finish_all)

        with nc.Block() as block:
            @block.sync
            def _(e):
                plan.run("sp", e)

            @block.gpsimd
            def _(e):
                plan.run("pool", e)

            @block.scalar
            def _(e):
                plan.run("act", e)

            @block.vector
            def _(e):
                plan.run("dve", e)

            @block.tensor
            def _(e):
                plan.run("pe", e)


_INS = ["x", "ctx_512", "L0_xattn_q_norm_w", "L0_xattn_k_norm_w", "L0_xattn_w_out", "L0_ffn_w_router",
        "L0_ffn_w_gate", "L0_ffn_w_up", "L0_ffn_w_down", "L0_ffn_amplitudes", "L0_ffn_expert_scale",
        "L0_ffn_shared_w_gate", "L0_ffn_shared_w_up", "L0_ffn_shared_w_down"]


def _rope_tables(length, width):
    import numpy as np
    exponent = np.arange(0, width, 2, dtype=np.float32) / np.float32(width)
    inv_freq = (np.float32(1.0) / np.power(np.float32(10000.0), exponent)).astype(np.float32)
    freqs = np.outer(np.arange(length, dtype=np.float32), inv_freq).astype(np.float32)
    cos, sin = np.cos(freqs), np.sin(freqs)
    return (np.concatenate([cos, cos], -1).astype(np.float32),
            np.concatenate([-sin, sin], -1).astype(np.float32))


def kernel(**inputs):
    import numpy as np
    import concourse.bacc as bacc
    from concourse.bass_utils import run_bass_kernel_spmd

    nc = bacc.Bacc("TRN2", target_bir_lowering=False, num_devices=1)
    arrays, args = {}, []
    given = [(name, np.ascontiguousarray(inputs[name])) for name in _INS]
    cos, sin = _rope_tables(512, 32)
    for name, a in given + [("rope_cos", cos), ("rope_sin", sin)]:
        arrays[f"in_{name}"] = a
        args.append(nc.dram_tensor(f"in_{name}", a.shape, mybir.dt.from_np(a.dtype),
                                   kind="ExternalInput").ap())
    shape = given[0][1].shape
    args.append(nc.dram_tensor("out", shape, mybir.dt.float32, kind="ExternalOutput").ap())
    attention_and_mixture_kernel(nc, *args)
    r = run_bass_kernel_spmd(nc, [arrays], core_ids=[0])
    return r.results[0]["out"]
```

```python
import math
from contextlib import ExitStack

import concourse.bass as bass
from concourse import mybir


TICK = ("fill_pe_1", "fill_dve_3", "scores_x", "pass_a_0", "fill_dve_1", "fill_pe_1", "pass_a_1",
        "scores_y", "fill_dve_1", "fill_pe_2", "row_max_0", "row_max_1", "fill_pe_1", "low_x",
        "fill_pe_1", "value_product", "pass_a_2", "fill_pe_1", "fill_dve_1", "value_rows",
        "fill_pe_2", "row_max_2", "pass_a_3", "row_max_3", "low_y")
AHEAD = {"pass_a": 7}
BEHIND = {"low_part": 1, "value_product": 2}
BACKLOG = 0
AT = dict(key_squares=-18, moments=-15, key_scale=-15, query_scale=-12, center=-14, rope_keys=-15,
          values=-8, turn_keys=-13, rope_queries=-12, turn_queries=-10, maxima_split=-4,
          maxima_turned=-2, combine=6, turn_out=8, project=5, output_weights=5, chunk_weights=56,
          router_weights=68, moments2=60)
LATER_TURN = 0
FIRST_MAXIMA = 0
FIRST_ROPES = {0: ("dve", "dve", "pool", "pool"),
               1: ("dve", "dve", "pool", "dve"),
               2: ("dve", "pool", "dve", "pool")}
POOL_LOW_PARTS = 2
FFN_START = 10
FFN_LEAD = 12
FFN_AHEAD = dict(normalize=10, turn_x=9, route=5, choose=4, choose_rest=3, turn_choice=1,
                 mix_weights=1)
FFN_TAIL = dict(turn_out=-8, project=-8)


class Plan:

    def __init__(self):
        self.steps = {"pe": [], "act": [], "dve": [], "pool": [], "sp": []}
        self.reached = {}
        self.sems = {}
        self.waited = {}

    def add(self, lane, name, issue):
        assert name not in self.reached, name
        self.steps[lane].append((issue, True))
        self.reached[name] = (self.sems[lane], sum(marks for _, marks in self.steps[lane]))

    def load(self, name, stream, count, issue):
        assert name not in self.reached, name
        sem, total = self.sems[stream]
        total += 16 * count
        self.sems[stream] = (sem, total)
        self.steps["sp"].append((lambda e, s=sem: issue(e, s), False))
        self.reached[name] = (sem, total)

    def need(self, engine, *names):
        for name in names:
            sem, count = self.reached[name]
            key = (id(engine), id(sem))
            if self.waited.get(key, 0) < count:
                engine.wait_ge(sem, count)
                self.waited[key] = count

    def run(self, lane, engine):
        for issue, marks in self.steps[lane]:
            last = issue(engine)
            if marks:
                last.then_inc(self.sems[lane], 1)


def attention_and_mixture_kernel(nc, x, ctx_in, q_norm_w, k_norm_w, w_out, w_router, w_gate, w_up,
                                 w_down, amplitudes, expert_scale, shared_w_gate, shared_w_up,
                                 shared_w_down, rope_cos, rope_sin, out):
    F32, F32R, BF16, F16, U32 = (mybir.dt.float32, mybir.dt.float32r, mybir.dt.bfloat16,
                                 mybir.dt.float16, mybir.dt.uint32)
    ALU, ACT, AX = mybir.AluOpType, mybir.ActivationFunctionType, mybir.AxisListType
    P = 128
    B, T, C = x.shape
    KVW = ctx_in.shape[2]
    D = rope_cos.shape[1]
    HALF = D // 2
    KV = KVW // D
    G = C // D // KV
    TT = T // P
    NT = B * TT
    KC = C // P
    NC = B * KV
    NH = NC * G
    NE = w_router.shape[1]
    I = w_down.shape[0]
    NK = w_gate.shape[1] // I
    NS = shared_w_gate.shape[1] // I
    NW = NK + NS
    ND = (I + NS * I) // P
    TOPK = 4
    EPS = 1e-5
    EPS_FFN = 1e-8
    SCALE = 1.0 / math.sqrt(D)
    NEG = -1e30
    PBIAS = math.log(256.0)
    PARTS = 3 * D
    VS = PARTS + 2
    MAXROW = 3 * D
    ROWS = MAXROW + 2
    QR, KR = 3, 8
    PR = 3
    LEAD = AHEAD["pass_a"]
    BASE = [sum(T - P * j for j in range(k)) for k in range(TT)]
    PW = sum(T - P * k for k in range(TT))
    XW = BASE[2]
    YW = PW - XW

    plan = Plan()
    need, add = plan.need, plan.add
    common = ExitStack()
    with common:
        used = {}

        def region(stack, name):
            used[name] = 0

            def place(label, shape, dt=F32):
                size = {F32: 4, F32R: 4, U32: 4, BF16: 2, F16: 2}[dt]
                used[name] += -(-size * math.prod(shape[1:]) // 32) * 32
                return stack.enter_context(nc.sbuf_tensor(label, shape, dt))
            return place

        def pad(stack, name, target):
            gap = used[target] - used[name]
            assert gap >= 0, (name, used)
            if gap:
                stack.enter_context(nc.sbuf_tensor(f"{name}_pad", [P, gap // 4], F32))

        sb = region(common, "common")
        x1 = sb("x1", [P, NT, C])
        raw = sb("raw", [P, KC, 2 * I])
        ident = sb("ident", [P, P])
        mixs = sb("mixs", [NE, NK])
        amp = sb("amp", [NE, NK, 2])
        amp_s = sb("amp_s", [NE, NK])
        es = sb("es", [NE, 4])
        cst = sb("cst", [P, 16])
        half_neg = cst[:, 0:8]
        log256 = cst[:, 8:9]
        neg_mean = cst[:, 12:16]
        st2 = sb("st2", [P, NT, 6])
        mv2 = sb("mv2", [P, NT, 2])
        ln2 = sb("ln2", [P, 4, NT])

        att_mem = ExitStack()
        ffn_mem = ExitStack()

        sb = region(att_mem, "att_early")
        cos_t = sb("cos_t", [P, TT, D])
        sin_t = sb("sin_t", [P, TT, D])
        junk = sb("junk", [P, TT, KVW], BF16)
        wq_b = sb("wq_b", [P, C])
        wk_b = sb("wk_b", [P, KVW])
        xc = sb("xc", [P, TT, C])
        ct = sb("ct", [P, 2, TT, KVW])
        stats = sb("stats", [P, 2, TT, 6])
        mv = sb("mv", [P, 2, TT, 2])
        ssk = sb("ssk", [P, 2, TT])
        sc = sb("sc", [P, 2, 8, TT])
        csq = sb("csq", [P, 2, 2, 2, TT, D])
        rw_b = sb("rw_b", [P, TT, P])
        r1_b = sb("r1_b", [P, 2, TT, P])
        r2_b = sb("r2_b", [P, TT, P])
        turned_h = sb("turned_h", [P, 2, T], F32R)
        turned_l = sb("turned_l", [P, 2, T], F32R)
        vr = sb("vr", [P, TT, KVW])
        sb = region(att_mem, "att_middle")
        ident16 = sb("ident16", [P, P], BF16)
        mask_kq = sb("mask_kq", [P, P], BF16)
        mask_qk = sb("mask_qk", [P, T])
        q_st = sb("q_st", [ROWS, QR, G, T], F32R)
        k_st = sb("k_st", [ROWS, KR, T], F32R)
        vp = sb("vp", [P, 2, TT, KV, VS], BF16)
        mx = sb("mx", [P, 2, TT, G])
        mhl = sb("mhl", [P, 2, TT, 2 * G], F32R)
        m_t = sb("m_t", [2 * G, T], F32R)
        p32 = sb("p32", [P, 2, PW])
        p_h = sb("p_h", [P, PR, PW], F16)
        p_l = sb("p_l", [P, PR, PW], F16)
        sb = region(att_mem, "att_late")
        osb = sb("osb", [P, 2, G, TT, VS])
        rinv = sb("rinv", [P, 2, G, TT])
        att = sb("att", [P, TT, P])
        o_h = sb("o_h", [P, KV, T], F32R)
        o_l = sb("o_l", [P, KV, T], F32R)
        wo_h = sb("wo_h", [P, KC, C], F32R)
        wo_l = sb("wo_l", [P, KC, C], F32R)
        att_mem.close()

        sb = region(ffn_mem, "ffn_early")
        w_h0 = sb("w_h0", [P, KC, 2 * I], F32R)
        w_l0 = sb("w_l0", [P, KC, 2 * I], F32R)
        hs = sb("hs", [P, 2, NS * I])
        first_mem = ExitStack()
        sb1 = region(first_mem, "first")
        rt_w = sb1("rt_w", [P, KC, 2 * NE], F32R)
        xn = sb1("xn", [P, 2, C])
        lg = sb1("lg", [P, 2, 2, NE + 8])
        ex = sb1("ex", [P, 2, 2, NE])
        cf = sb1("cf", [P, 2, 2, NE + 8])
        cf_t = sb1("cf_t", [NE, 2, 2, P])
        sm = sb1("sm", [P, 2, 8, 2])
        top = sb1("top", [P, 2, 2, 8])
        top4 = sb1("top4", [P, 2, 2, 8])
        first_mem.close()
        sb = region(ffn_mem, "last")
        ws_h = sb("ws_h", [P, NS * I // P, C], F32R)
        ws_l = sb("ws_l", [P, NS * I // P, C], F32R)
        pad(ffn_mem, "last", "first") if used["first"] > used["last"] else None
        used["ffn_early"] += max(used["first"], used["last"])
        pad(ffn_mem, "ffn_early", "att_early")
        sb = region(ffn_mem, "ffn_middle")
        t_h = sb("t_h", [P, KC, NT * P], F32R)
        t_l = sb("t_l", [P, KC, NT * P], F32R)
        th = sb("th", [P, 2, I])
        ga = sb("ga", [P, 2, I])
        gb = sb("gb", [P, 2, I])
        wt = sb("wt", [P, NT, NK])
        wd_h = sb("wd_h", [P, I // P, C], F32R)
        pad(ffn_mem, "ffn_middle", "att_middle")
        sb = region(ffn_mem, "ffn_late")
        macc = sb("macc", [P, NT, I])
        w_h1 = sb("w_h1", [P, KC, 2 * I], F32R)
        w_l1 = sb("w_l1", [P, KC, 2 * I], F32R)
        d_h = sb("d_h", [P, 2, ND, P], F32R)
        d_l = sb("d_l", [P, 2, ND, P], F32R)
        wd_l = sb("wd_l", [P, I // P, C], F32R)
        ffn_mem.close()
        w_hs, w_ls = (w_h0, w_h1), (w_l0, w_l1)

        pair = common.enter_context(nc.psum_tensor("pair", [P, 1024], F32))
        bank = [common.enter_context(nc.psum_tensor(f"bank{i}", [P, 512], F32)) for i in range(6)]
        a_bank = bank[0:2]
        b_bank = bank[2]
        v_bank = bank[3]
        m_bank = bank[4:6]
        g_bank = [pair[:, 0:512], pair[:, 512:1024], bank[0], bank[1]]
        f_bank = [bank[2], bank[3]]

        def sem(name):
            return common.enter_context(nc.semaphore(name))

        for lane in plan.steps:
            plan.sems[lane] = sem(f"{lane}_done")
        for stream in (["consts", "wo", "amps", "out0", "out1", "raw0", "raw1", "m0", "m1"]
                       + [f"x{t}" for t in range(TT)] + [f"x_b{b}" for b in range(1, B)] + ["c_b0", "c_b1"]
                       + [f"q{i}_{j}" for i in range(QR) for j in range(G)] + [f"k{i}" for i in range(KR)]):
            plan.sems[stream] = (sem(f"{stream}_landed"), 0)

        f32 = lambda ap: ap.bitcast(F32)

        queue = []

        def fill(name, issue):
            queue.append((name, issue))

        def fill_gap(steps=1):
            for _ in range(min(steps, len(queue))):
                add("dve", *queue.pop(0))

        pe_queue = []

        def fill_pe(steps=1):
            for _ in range(min(steps, len(pe_queue))):
                pe_queue.pop(0)()

        def settle(name):
            while any(name == waiting for waiting, _ in queue):
                fill_gap()

        def constants():
            def small(e):
                e.memset(half_neg, -0.5)
                return e.memset(log256, PBIAS)
            add("pool", "consts", small)

            def zeros(e):
                e.memset(ident[:], 0.0)
                e.memset(ident16[:], 0.0)
                e.memset(mask_kq[:], 0.0)
                return e.memset(mask_qk[:], 0.0)
            add("pool", "zeroed", zeros)

            def shapes(e):
                need(e, "zeroed")
                for m in (ident, ident16):
                    e.affine_select(out=m[:], in_=m[:], compare_op=ALU.not_equal, fill=1.0, base=0,
                                    pattern=[[-1, P]], channel_multiplier=1)
                e.affine_select(out=mask_kq[:], in_=mask_kq[:], compare_op=ALU.is_ge, fill=NEG,
                                base=0, pattern=[[1, P]], channel_multiplier=-1)
                tri = mask_qk[:, T - P:T]
                return e.affine_select(out=tri, in_=tri, compare_op=ALU.is_ge, fill=NEG,
                                       base=0, pattern=[[-1, P]], channel_multiplier=1)
            add("pool", "masks", shapes)

            def ones_v(e):
                for r in range(2):
                    last = e.memset(vp[:, r, :, :, PARTS:VS], 1.0)
                return last
            add("pool", "ones_v", ones_v)

            def ones(e):
                return e.memset(f32(k_st[MAXROW:ROWS, 0:KR // 2, :]), 1.0)
            add("dve", "ones", ones)

            def more_ones(e):
                return e.memset(f32(k_st[MAXROW:ROWS, KR // 2:KR, :]), 1.0)
            constants.more_ones = more_ones

        def load_batch(b, what):
            r = b % 2

            def load_ctx(e, s):
                if b >= 2:
                    need(e, ("v3", b - 2), ("rope_w", b - 2, 0))
                e.dma_start(ct[:, r], ctx_in[b].rearrange("(t p) n -> p t n", p=P)).then_inc(s, 16)

            def load_x(e, s):
                e.dma_start(x1[:, b * TT:(b + 1) * TT, :],
                            x[b].rearrange("(t p) n -> p t n", p=P)).then_inc(s, 16)

            def tile_of_x(t):
                def go(e, s):
                    e.dma_start(x1[:, t, :], x[b, t * P:(t + 1) * P, :]).then_inc(s, 16)
                return go

            if what == "ctx":
                plan.load(("ctx", b), f"c_b{r}", 1, load_ctx)
            elif b == 0:
                for t in range(TT):
                    plan.load(("x", b, t), f"x{t}", 1, tile_of_x(t))
            else:
                plan.load(("x", b, 0), f"x_b{b}", 1, load_x)
                for t in range(1, TT):
                    plan.reached[("x", b, t)] = plan.reached[("x", b, 0)]

        def load_constants(e, s):
            e.dma_start(cos_t[:], rope_cos.rearrange("(t p) d -> p t d", p=P)).then_inc(s, 16)
            e.dma_start(sin_t[:], rope_sin.rearrange("(t p) d -> p t d", p=P)).then_inc(s, 16)
            e.dma_start(wk_b[:], k_norm_w.partition_broadcast(P)).then_inc(s, 16)
            e.dma_start(wq_b[:], q_norm_w.partition_broadcast(P)).then_inc(s, 16)

        def key_squares(b):
            r = b % 2
            for t in range(TT):
                def ssq(e, t=t):
                    need(e, ("ctx", b))
                    if b >= 2:
                        need(e, ("k_eps", b - 2))
                    if b >= 1:
                        need(e, ("ssq", b - 1, t))
                    return e.tensor_tensor_reduce(junk[:, t, :], ct[:, r, t, :], ct[:, r, t, :],
                                                  1.0 / KVW, 0.0, ALU.mult, ALU.add, ssk[:, r, t:t + 1])
                fill(("ssq", b, t), ssq)

        def key_scale(b):
            r = b % 2
            settle(("ssq", b, TT - 1))
            k_eps, r_k = sc[:, r, 1, :], sc[:, r, 3, :]

            def eps(e):
                need(e, ("ssq", b, TT - 1), "consts")
                if b >= 2:
                    need(e, ("k_tables", b - 2))
                return e.tensor_scalar(k_eps, ssk[:, r, :], EPS, None, ALU.add)
            add("pool", ("k_eps", b), eps)

            def power(e):
                need(e, ("k_eps", b))
                return e.tensor_tensor(r_k, k_eps, half_neg[:, 0:TT], ALU.pow)
            add("pool", ("k_pow", b), power)
            scaled_tables(b, "k", 1, r_k, ("k_pow", b), ("rope", b - 2, 0))

        def moments(b):
            r = b % 2
            for t in range(TT):
                def bn(e, t=t):
                    need(e, ("x", b, t))
                    return e.bn_stats(stats[:, r, t, :], x1[:, b * TT + t, :])
                fill(("bn", b, t), bn)
            for t in range(TT):
                def agg(e, t=t):
                    need(e, ("bn", b, t))
                    if b >= 2 and t == 0:
                        need(e, ("eps2", b - 2), ("center", b - 2, TT - 1))
                    return e.bn_aggr(mv[:, r, t, :], stats[:, r, t, :])
                fill(("agg", b, t), agg)

        def center_x(b):
            r = b % 2
            if b == 0:
                settle(("agg", b, TT - 1))

                def negate(e):
                    need(e, ("agg", b, TT - 1))
                    return e.tensor_scalar(neg_mean, mv[:, r, :, 0], -1.0, None, ALU.mult)
                add("pool", "neg_mean", negate)
                for t in range(TT):
                    def shift(e, t=t):
                        need(e, "neg_mean")
                        return e.activation(xc[:, t, :], x1[:, t, :], ACT.Identity,
                                            bias=neg_mean[:, t:t + 1])
                    add("act", ("center", b, t), shift)
                return
            for t in range(TT):
                def center(e, t=t):
                    need(e, ("agg", b, t))
                    if b >= 1:
                        need(e, ("rope_w", b - 1, KV))
                    return e.tensor_scalar(xc[:, t, :], x1[:, b * TT + t, :], mv[:, r, t, 0:1], None,
                                           ALU.subtract)
                fill(("center", b, t), center)

        def query_scale(b):
            r = b % 2
            settle(("agg", b, TT - 1))
            var = mv[:, r, :, 1]
            v_eps, r_ln, v1, v2, s_rms, s_q = (sc[:, r, i, :] for i in (0, 2, 4, 5, 6, 7))

            def eps1(e):
                need(e, ("agg", b, TT - 1), "consts")
                if b >= 2:
                    need(e, ("q_tables", b - 2))
                return e.tensor_scalar(v_eps, var, EPS, None, ALU.add)
            add("pool", ("eps1", b), eps1)

            def pow_a(e):
                need(e, ("eps1", b), "consts")
                return e.tensor_tensor(r_ln, v_eps, half_neg[:, 0:TT], ALU.pow)
            add("pool", ("pow_b", b), pow_a)

            def sq1(e):
                need(e, ("pow_b", b))
                return e.tensor_tensor(v1, var, r_ln, ALU.mult)
            add("pool", ("sq1", b), sq1)

            def sq2(e):
                need(e, ("sq1", b))
                return e.tensor_tensor(v2, v1, r_ln, ALU.mult)
            add("pool", ("sq2", b), sq2)

            def eps2(e):
                need(e, ("sq2", b))
                return e.tensor_scalar(v1, v2, EPS, None, ALU.add)
            add("pool", ("eps2", b), eps2)

            def pow_q(e):
                need(e, ("eps2", b))
                return e.tensor_tensor(s_rms, v1, half_neg[:, 0:TT], ALU.pow)
            add("pool", ("pow_q", b), pow_q)

            def scale_q(e):
                need(e, ("pow_q", b))
                return e.tensor_tensor(s_q, s_rms, r_ln, ALU.mult)
            add("pool", ("scale_q", b), scale_q)

            scaled_tables(b, "q", 0, s_q, ("scale_q", b), ("rope", b - 2, KV))

        def scaled_tables(b, name, i, scale, ready, last_use):
            def tables(e):
                need(e, ready, "tables_in")
                if b >= 2:
                    need(e, last_use)
                for j, tab in enumerate((cos_t, sin_t)):
                    last = e.tensor_tensor(csq[:, b % 2, i, j], tab[:],
                                           scale.unsqueeze(2).broadcast_to([P, TT, D]), ALU.mult)
                return last
            add("dve" if b == 0 else "pool", (name + "_tables", b), tables)

        def rope(b, i):
            r, n = b % 2, b * (KV + 1) + i
            q = n % 2
            src = ct[:, r] if i == 0 else xc[:, :, (i - 1) * P:i * P]
            w = wk_b[:] if i == 0 else wq_b[:, (i - 1) * P:i * P]
            cs, sn = csq[:, r, 1 if i == 0 else 0, 0], csq[:, r, 1 if i == 0 else 0, 1]
            wb = w.unsqueeze(1).broadcast_to([P, TT, P])
            heads = lambda ap: ap.rearrange("p t (h d) -> p t h d", d=D)
            lane = FIRST_ROPES.get(n, ("pool",) * 4)
            prev = n - 2
            pb, pi = prev // (KV + 1), prev % (KV + 1)
            if i == 1:
                settle(("center", b, TT - 1))

            def weigh(e):
                if i == 0:
                    need(e, ("ctx", b), "tables_in")
                else:
                    need(e, ("center", b, TT - 1), "tables_in")
                if n >= 1:
                    need(e, ("rope", (n - 1) // (KV + 1), (n - 1) % (KV + 1)))
                return e.tensor_tensor(rw_b[:], src, wb, ALU.mult)
            add(lane[0], ("rope_w", b, i), weigh)

            def cosine(e):
                need(e, ("rope_w", b, i), ("k_tables" if i == 0 else "q_tables", b))
                if prev >= 0:
                    need(e, ("turn", pb, pi))
                return e.tensor_tensor(heads(r1_b[:, q]), heads(rw_b[:]),
                                       cs.unsqueeze(2).broadcast_to([P, TT, P // D, D]), ALU.mult)
            add(lane[1], ("rope_c", b, i), cosine)

            def sine(e):
                need(e, ("rope_w", b, i), ("k_tables" if i == 0 else "q_tables", b))
                for lo, hi in ((0, HALF), (HALF, 0)):
                    last = e.tensor_tensor(
                        heads(r2_b[:])[:, :, :, lo:lo + HALF], heads(rw_b[:])[:, :, :, hi:hi + HALF],
                        sn[:, :, lo:lo + HALF].unsqueeze(2).broadcast_to([P, TT, P // D, HALF]), ALU.mult)
                return last
            add(lane[2], ("rope_s", b, i), sine)

            def total(e):
                need(e, ("rope_c", b, i), ("rope_s", b, i))
                return e.tensor_tensor(r1_b[:, q], r1_b[:, q], r2_b[:], ALU.add)
            add(lane[3], ("rope", b, i), total)

        m_items = []

        def take_m_bank(reader):
            m_items.append(reader)
            n = len(m_items) - 1
            if n >= 2:
                settle(m_items[n - 2])
            return m_bank[n % 2], (m_items[n - 2] if n >= 2 else None)

        def turn_in(b, i):
            n = b * (KV + 1) + i
            q = n % 2
            dst, before = take_m_bank(("turned_l", b, i))

            def turn(e):
                need(e, ("rope", b, i), "masks")
                if before:
                    need(e, before)
                for t in range(TT):
                    last = e.transpose(dst[:, t * P:(t + 1) * P], r1_b[:, q, t, :], ident[:])
                return last
            add("pe", ("turn", b, i), turn)

            def split_h(e):
                need(e, ("turn", b, i))
                if n >= 2:
                    need(e, ("stacked", n - 2))
                return e.activation(turned_h[:, q, :], dst[:], ACT.Copy)
            add("act", ("turned_h", b, i), split_h)

            def split_l(e):
                need(e, ("turned_h", b, i))
                if n >= 2:
                    need(e, ("stacked", n - 2))
                return e.tensor_tensor(turned_l[:, q, :], dst[:], f32(turned_h[:, q, :]), ALU.subtract)
            fill(("turned_l", b, i), split_l)
            if n == 1:
                fill("more_ones", constants.more_ones)

            def stack_keys(j):
                c, q = b * KV + j, b * (KV + 1) % 2

                def stack_k(e, s):
                    need(e, ("turned_l", b, 0))
                    if c >= KR:
                        need(e, ("pass_bx", (c - KR) * G + G - 1), ("pass_by", (c - KR) * G + G - 1))
                    for row, part in ((0, turned_h), (D, turned_l), (2 * D, turned_h)):
                        e.dma_start(f32(k_st[row:row + D, c % KR, :]),
                                    f32(part[j * D:(j + 1) * D, q, :])).then_inc(s, 16)
                plan.load(("k_st", c), f"k{c % KR}", 3, stack_k)

            if i == 0:
                stack_keys(0)
            else:
                c = b * KV + i - 1

                for j in range(G):
                    def stack_q(e, s, j=j):
                        need(e, ("turned_l", b, i))
                        if c >= QR:
                            need(e, ("pass_bx", (c - QR) * G + G - 1), ("pass_by", (c - QR) * G + G - 1))
                        for row, part in ((0, turned_h), (D, turned_h), (2 * D, turned_l)):
                            e.dma_start(f32(q_st[row:row + D, c % QR, j, :]),
                                        f32(part[j * D:(j + 1) * D, q, :])).then_inc(s, 16)
                    plan.load(("q_st", c * G + j), f"q{c % QR}_{j}", 3, stack_q)
            if i == 1:
                for j in range(1, KV):
                    stack_keys(j)
            stacked = ([("k_st", b * KV + j) for j in range(KV)] if i == 0 else
                       [("q_st", c * G + j) for j in range(G)])
            aliases[("stacked", n)] = stacked

        def values(b):
            r = b % 2
            put = fill if b == 0 else lambda *step: add("pool", *step)
            part = lambda k: vp[:, r, :, :, k * D:(k + 1) * D]
            heads = lambda ap: ap.rearrange("p t (h d) -> p t h d", d=D)

            def v1(e):
                need(e, ("ctx", b))
                if b >= 2:
                    need(e, ("pv", (b - 1) * KV * G - 1))
                return e.tensor_copy(part(0), heads(ct[:, r]))
            put(("v1", b), v1)

            def rest(e):
                need(e, ("v1", b))
                return e.tensor_tensor(heads(vr[:]), heads(ct[:, r]), part(0), ALU.subtract)
            put(("vr", b), rest)

            def v2(e):
                need(e, ("vr", b))
                return e.tensor_copy(part(1), heads(vr[:]))
            put(("v2", b), v2)

            def v3(e):
                need(e, ("v2", b))
                return e.tensor_tensor(part(2), heads(vr[:]), part(1), ALU.subtract)
            put(("v3", b), v3)

        def pass_a(n, t):
            c, j = n // G, n % G
            i = n * TT + t

            def scores(e):
                need(e, ("k_st", c), ("q_st", n))
                if i >= 2:
                    need(e, ("max", (i - 2) // TT, (i - 2) % TT))
                w = max((t + 1) * P, 2 * P)
                return e.matmul(a_bank[i % 2][:, 0:w], q_st[0:MAXROW, c % QR, j, t * P:(t + 1) * P],
                                k_st[0:MAXROW, c % KR, 0:w], start=True, stop=True)
            add("pe", ("pass_a", n, t), scores)

        def row_max(n, t):
            c, j = n // G, n % G
            s, width = a_bank[(n * TT + t) % 2], (t + 1) * P

            def largest(e):
                need(e, ("pass_a", n, t), "masks")
                if c >= 2 and j == 0:
                    need(e, ("m_lo", c - 2))
                return e.tensor_tensor_reduce(s[:, 0:width], s[:, 0:width], mask_qk[:, T - width:T],
                                              1.0, -3e38, ALU.add, ALU.max, mx[:, c % 2, t, j:j + 1])
            add("dve", ("max", n, t), largest)

        def maxima(c, part):
            r = c % 2
            hi, lo = mhl[:, r, :, 0:G], mhl[:, r, :, G:2 * G]

            def m_hi(e):
                need(e, *[("max", c * G + G - 1, t) for t in range(TT)])
                if c >= 2:
                    need(e, ("m_turn", c - 2))
                return e.tensor_scalar(hi, mx[:, r], -1.0, None, ALU.mult)
            if part == "split":
                add("dve", ("m_hi", c), m_hi)

            def m_lo(e):
                need(e, ("m_hi", c))
                return e.scalar_tensor_tensor(lo, mx[:, r], -1.0, f32(hi), ALU.mult, ALU.subtract)
            if part == "split":
                add("dve", ("m_lo", c), m_lo)
                return
            dst, before = take_m_bank(("m_t", c))

            def m_turn(e):
                need(e, ("m_lo", c), "masks")
                if before:
                    need(e, before)
                for t in range(TT):
                    last = e.transpose(dst[0:2 * G, t * P:(t + 1) * P], f32(mhl[:, r, t, :]), ident[:])
                return last
            add("pe", ("m_turn", c), m_turn)

            def m_out(e):
                need(e, ("m_turn", c))
                if c >= 1:
                    need(e, ("m_rows", c - 1))
                return e.activation(m_t[:], dst[0:2 * G, :], ACT.Copy)
            add("act", ("m_t", c), m_out)

            def rows(e, s):
                need(e, ("m_t", c))
                if c >= QR:
                    need(e, ("pass_bx", (c - QR) * G + G - 1), ("pass_by", (c - QR) * G + G - 1))
                for k in range(2):
                    e.dma_start(f32(q_st[MAXROW + k:MAXROW + k + 1, c % QR, :, :]),
                                f32(m_t[k * G:(k + 1) * G, :])).then_inc(s, 16)
            plan.load(("m_rows", c), f"m{r}", 2, rows)

        def pass_b(n, name):
            c, j, r, rp = n // G, n % G, n % 2, n % PR
            x_part = name == "x"
            src, at, width = (pair, 0, XW) if x_part else (b_bank, XW, YW)

            def tile_scores(e, k, out_ap, q0, mask_at):
                e.matmul(out_ap, k_st[:, c % KR, k * P:(k + 1) * P], q_st[:, c % QR, j, q0:T],
                         start=True, stop=True)
                return e.matmul(mask_at, ident16[:], mask_kq[:], start=False, stop=True,
                                skip_group_check=True)

            def scores(e):
                need(e, ("m_rows", c), "masks", "ones", "more_ones")
                if n >= 1:
                    need(e, (f"exp_{name}16", n - 1))
                if x_part:
                    for k in range(2):
                        last = tile_scores(e, k, pair[:, BASE[k]:BASE[k] + T - k * P], k * P,
                                           pair[:, BASE[k]:BASE[k] + P])
                    return last
                tile_scores(e, 3, b_bank[:, P:3 * P], 2 * P, b_bank[:, 2 * P:3 * P])
                return tile_scores(e, 2, b_bank[:, 0:2 * P], 2 * P, b_bank[:, 0:P])
            add("pe", (f"pass_b{name}", n), scores)

            def exp32(e):
                need(e, (f"pass_b{name}", n), "consts")
                if n >= 2:
                    need(e, (f"p_l{name}", n - 2))
                return e.activation(p32[:, r, at:at + width], src[:, 0:width], ACT.Exp,
                                    bias=log256, scale=SCALE)
            add("act", (f"exp_{name}32", n), exp32)

            def exp16(e):
                if n >= PR:
                    need(e, ("pv", n - PR))
                return e.activation(p_h[:, rp, at:at + width], src[:, 0:width], ACT.Exp,
                                    bias=log256, scale=SCALE)
            add("act", (f"exp_{name}16", n), exp16)

        def low_part(n, name):
            r, rp = n % 2, n % PR
            cols = slice(0, XW) if name == "x" else slice(XW, PW)

            def low(e):
                need(e, (f"exp_{name}16", n))
                if n >= PR:
                    need(e, ("pv", n - PR))
                return e.tensor_tensor(p_l[:, rp, cols], p32[:, r, cols], p_h[:, rp, cols], ALU.subtract)
            add("pool" if name == "y" and n % G < POOL_LOW_PARTS else "dve", (f"p_l{name}", n), low)

        def value_product(n):
            c, j, rp = n // G, n % G, n % PR
            b, kv = c // KV, c % KV

            def pv(e):
                need(e, ("p_lx", n), ("p_ly", n), ("v3", b), "ones_v")
                if n >= 1:
                    need(e, ("osb", n - 1))
                for t in range(TT):
                    for k in range(t + 1):
                        for m, p in enumerate((p_h, p_l)):
                            at = BASE[k] + (t - k) * P
                            last = e.matmul(v_bank[:, t * VS:t * VS + VS - 1], p[:, rp, at:at + P],
                                            vp[:, b % 2, k, kv, 0:VS - 1],
                                            start=(k == 0 and m == 0), stop=(k == t and m == 1))
                return last
            add("pe", ("pv", n), pv)

        def value_rows(n):
            c, j = n // G, n % G

            def evacuate(e):
                need(e, ("pv", n))
                if c >= 2 and j == 0:
                    need(e, ("norm", c - 2))
                src = v_bank[:, 0:TT * VS].rearrange("p (t v) -> p t v", v=VS)[:, :, 0:VS - 1]
                return e.activation(osb[:, c % 2, j, :, 0:VS - 1], src, ACT.Copy)
            add("act", ("osb", n), evacuate)

        def combine(c):
            r = c % 2
            lane = "pool" if c < NC - 1 else "dve"
            part = lambda k: osb[:, r, :, :, k * D:(k + 1) * D]
            dst = att[:].rearrange("p t (h d) -> p h t d", d=D)

            def inverse(e):
                need(e, ("osb", c * G + G - 1))
                if c >= 2:
                    need(e, ("norm", c - 2))
                return e.reciprocal(rinv[:, r], osb[:, r, :, :, PARTS])
            add("dve", ("rinv", c), inverse)

            def add12(e):
                need(e, ("osb", c * G + G - 1))
                return e.tensor_tensor(part(0), part(0), part(1), ALU.add)
            add(lane, ("add12", c), add12)

            def add3(e):
                need(e, ("add12", c))
                return e.tensor_tensor(part(0), part(0), part(2), ALU.add)
            add(lane, ("add3", c), add3)

            def norm(e):
                need(e, ("add3", c), ("rinv", c))
                if c >= 1:
                    need(e, ("o_turn", c - 1))
                return e.tensor_tensor(dst, part(0), rinv[:, r].unsqueeze(3).broadcast_to([P, G, TT, D]),
                                       ALU.mult)
            add(lane, ("norm", c), norm)

        def turn_out(c):
            r, kv, b = c % 2, c % KV, c // KV
            dst_m, before = take_m_bank(("o_l", c))

            def turn(e):
                need(e, ("norm", c), before)
                for t in range(TT):
                    last = e.transpose(dst_m[:, t * P:(t + 1) * P], att[:, t, :], ident[:])
                return last
            add("pe", ("o_turn", c), turn)

            def split_h(e):
                need(e, ("o_turn", c))
                if b >= 1:
                    need(e, ("proj", b * TT - 1))
                return e.activation(o_h[:, kv, :], dst_m[:], ACT.Copy)
            add("act", ("o_h", c), split_h)

            def split_l(e):
                need(e, ("o_h", c))
                if b >= 1:
                    need(e, ("proj", b * TT - 1))
                return e.tensor_tensor(o_l[:, kv, :], dst_m[:], f32(o_h[:, kv, :]), ALU.subtract)
            fill(("o_l", c), split_l)

        def project(g, k):
            b, t = g // TT, g % TT
            if k == 0:
                settle(("o_l", b * KV + KV - 1))
                project.bank = take_m_bank(("x1", g))
            dst, before = project.bank

            def proj(e):
                need(e, ("o_l", b * KV + KV - 1), before, ("wo_l", KC - 1))
                rows = slice(t * P, (t + 1) * P)
                for m, (o, w) in enumerate(((o_h, wo_h), (o_h, wo_l), (o_l, wo_h))):
                    last = e.matmul(dst[:], o[:, k, rows], w[:, k, :], start=(k == 0 and m == 0),
                                    stop=(k == KC - 1 and m == 2))
                return last
            add("pe", ("proj", g) if k == KC - 1 else ("proj", g, k), proj)
            if k < KC - 1:
                return

            def residual(e):
                need(e, ("proj", g), ("center", b, t))
                return e.tensor_tensor(x1[:, g, :], x1[:, g, :], dst[:], ALU.add)
            fill(("x1", g), residual)

        def output_weights(what):
            def load(e, s):
                e.dma_start(raw[:], w_out.rearrange("(t p) n -> p t n", p=P)).then_inc(s, 16)
            if what == "load":
                plan.load("wo_raw", "wo", 1, load)
                return
            k = what
            dst, before = take_m_bank(("wo_l", k))

            def turn(e):
                need(e, "wo_raw", "masks")
                if before:
                    need(e, before)
                for t in range(KC):
                    last = e.transpose(dst[:, t * P:(t + 1) * P], raw[:, t, k * P:(k + 1) * P],
                                       ident[:])
                return last
            add("pe", ("wo_turn", k), turn)

            def split_h(e):
                need(e, ("wo_turn", k))
                return e.activation(wo_h[:, k, :], dst[:], ACT.Copy)
            add("act", ("wo_h", k), split_h)

            def split_l(e):
                need(e, ("wo_h", k))
                return e.tensor_tensor(wo_l[:, k, :], dst[:], f32(wo_h[:, k, :]), ALU.subtract)
            fill(("wo_l", k), split_l)

        def mixture_table(what):
            def load(e, s):
                e.dma_start(amp[:], amplitudes).then_inc(s, 16)
                e.dma_start(es[:, 0:1], expert_scale.rearrange("(e o) -> e o", o=1)).then_inc(s, 16)
            if what == "load":
                plan.load("amps", "amps", 2, load)
                return

            def square(e):
                need(e, "amps")
                return e.tensor_tensor(amp[:], amp[:], amp[:], ALU.mult)
            fill("amp_sq", square)

            def power(e):
                need(e, "amp_sq")
                return e.tensor_tensor(amp_s[:], amp[:, :, 0], amp[:, :, 1], ALU.add)
            fill("amp_s", power)

            def total(e):
                need(e, "amp_s")
                return e.tensor_reduce(es[:, 1:2], amp_s[:], AX.X, ALU.add)
            fill("amp_sum", total)

            def eps(e):
                need(e, "amp_sum")
                return e.tensor_scalar(es[:, 2:3], es[:, 1:2], EPS_FFN, None, ALU.add)
            fill("amp_eps", eps)

            def inverse(e):
                need(e, "amp_eps")
                return e.reciprocal(es[:, 3:4], es[:, 2:3])
            fill("amp_inv", inverse)

            def scaled(e):
                need(e, "amp_inv")
                return e.tensor_scalar(mixs[:], amp_s[:], es[:, 3:4], es[:, 0:1], ALU.mult, ALU.mult)
            fill("mixs", scaled)

        early_over = ([("k_st", NC - 1 - j) for j in range(KV)] + [("q_st", NH - 1 - j) for j in range(G)]
                      + [("v3", B - 1), ("rope", B - 1, KV)])
        middle_over = [("pv", NH - 1), ("p_lx", NH - 1), ("p_ly", NH - 1), ("m_rows", NC - 1)]
        late_over = [("proj", NT - 1), ("norm", NC - 1)]

        raw_uses = []

        def split_weights(name, source, dst_h, dst_l, slots, ready, put=lambda *step: add("dve", *step)):
            for h in range(0, slots, 2):
                n = len(raw_uses)
                side = n % 2
                src = raw[:, 2 * side:2 * side + min(2, slots - h), :]

                def load(e, s, h=h, n=n, src=src):
                    need(e, ("wo_turn", KC - 1))
                    if n >= 2:
                        need(e, raw_uses[n - 2])
                    for dst, part in source(h, src):
                        e.dma_start(dst, part).then_inc(s, 16)
                plan.load((name, "raw", h), f"raw{side}", len(source(h, src)), load)
                for k in range(h, min(h + 2, slots)):
                    def split_h(e, k=k, h=h, src=src):
                        need(e, (name, "raw", h), *ready)
                        return e.activation(dst_h(k), src[:, k - h, :], ACT.Copy)
                    add("act", (name, "h", k), split_h)

                    def split_l(e, k=k, h=h, src=src):
                        need(e, (name, "h", k), *ready)
                        return e.tensor_tensor(dst_l(k), src[:, k - h, :], f32(dst_h(k)), ALU.subtract)
                    put((name, "l", k), split_l)
                raw_uses.append((name, "l", min(h + 1, slots - 1)))

        def chunk_weights(w):
            gate, up, at = (w_gate, w_up, w * I) if w < NK else (shared_w_gate, shared_w_up, (w - NK) * I)

            def source(h, dst):
                view = lambda m: m[h * P:(h + 2) * P, at:at + I].rearrange("(k p) n -> p k n", p=P)
                return [(dst[:, :, 0:I], view(gate)), (dst[:, :, I:2 * I], view(up))]
            ready = [("unit", w - 2, NT - 1)] if w >= 2 else early_over if w == 0 else late_over
            split_weights(("w", w), source, lambda k: w_hs[w % 2][:, k, :], lambda k: w_ls[w % 2][:, k, :],
                          KC, ready, put=fill if w == 0 else lambda *step: add("dve", *step))

        def router_weights():
            n = len(raw_uses)
            side = n % 2
            src = raw[:, 2 * side, :].rearrange("p (k n) -> p k n", n=NE)

            def load(e, s):
                if n >= 2:
                    need(e, raw_uses[n - 2])
                need(e, ("wo_turn", KC - 1))
                e.dma_start(src, w_router.rearrange("(k p) n -> p k n", p=P)).then_inc(s, 16)
            plan.load("rt_raw", f"raw{side}", 1, load)

            def split_h(e):
                need(e, "rt_raw", *early_over)
                return e.activation(rt_w[:, :, 0:NE], src, ACT.Copy)
            add("act", "rt_h", split_h)

            def split_l(e):
                need(e, "rt_h")
                return e.tensor_tensor(rt_w[:, :, NE:2 * NE], src, f32(rt_w[:, :, 0:NE]), ALU.subtract)
            fill("rt_l", split_l)
            raw_uses.append("rt_l")

        def down_weights():
            def source_of(m):
                return lambda h, dst: [(dst, m[h * P:(h + 2) * P, :].rearrange("(k p) n -> p k n", p=P))]
            split_weights("wd", source_of(w_down), lambda k: wd_h[:, k, :], lambda k: wd_l[:, k, :],
                          I // P, late_over + middle_over)
            split_weights("ws", source_of(shared_w_down), lambda k: ws_h[:, k, :],
                          lambda k: ws_l[:, k, :], NS * I // P, [("wt", NT // 2 - 1), ("coeff", NT // 2 - 1)])

        f_items = [("exp_y16", NH - 1), ("osb", NH - 1)]
        g_items = [("exp_x16", NH - 1), ("exp_x16", NH - 1), ("max", NH - 1, TT - 2), ("max", NH - 1, TT - 1)]

        def take(items, banks, reader):
            items.append(reader)
            n = len(items) - 1
            settle(items[n - len(banks)])
            return banks[n % len(banks)], items[n - len(banks)]

        def moments2(g):
            def bn(e):
                need(e, ("x1", g))
                return e.bn_stats(st2[:, g, :], x1[:, g, :])
            fill(("bn2", g), bn)

            def agg(e):
                need(e, ("bn2", g))
                return e.bn_aggr(mv2[:, g, :], st2[:, g, :])
            fill(("agg2", g), agg)

        def norm_scales(b):
            ts = slice(b * TT, (b + 1) * TT)
            v_eps, rstd, prod, offset = (ln2[:, i, ts] for i in range(4))
            settle(("agg2", (b + 1) * TT - 1))

            def eps(e):
                need(e, ("agg2", (b + 1) * TT - 1))
                return e.tensor_scalar(v_eps, mv2[:, ts, 1], EPS, None, ALU.add)
            add("pool", ("eps3", b), eps)

            def power(e):
                need(e, ("eps3", b))
                return e.tensor_tensor(rstd, v_eps, half_neg[:, 0:TT], ALU.pow)
            add("pool", ("rstd", b), power)

            def product(e):
                need(e, ("rstd", b))
                return e.tensor_tensor(prod, mv2[:, ts, 0], rstd, ALU.mult)
            add("pool", ("mean_rstd", b), product)

            def negate(e):
                need(e, ("mean_rstd", b))
                return e.tensor_scalar(offset, prod, -1.0, None, ALU.mult)
            add("pool", ("offset", b), negate)

        def sentinels():
            def minus_one(e):
                need(e, *early_over)
                e.memset(lg[:, :, :, NE:NE + 8], -1.0)
                return e.memset(top4[:], -1.0)
            add("pool", "sentinels", minus_one)

        def normalize(g):
            r = g % 2

            def norm(e):
                need(e, ("offset", g // TT), *early_over)
                if g >= 2:
                    need(e, ("x_turn", g - 2))
                return e.activation(xn[:, r, :], x1[:, g, :], ACT.Identity, scale=ln2[:, 1, g:g + 1],
                                    bias=ln2[:, 3, g:g + 1])
            add("act", ("xn", g), norm)

        def turn_x(g):
            r = g % 2
            dst, before = take(f_items, f_bank, ("t_l", g))
            view = dst[:].rearrange("p (k n) -> p k n", n=P)
            cols = slice(g * P, (g + 1) * P)

            def turn(e):
                need(e, ("xn", g), before)
                for k in range(KC):
                    last = e.transpose(view[:, k, :], xn[:, r, k * P:(k + 1) * P], ident[:])
                return last
            add("pe", ("x_turn", g), turn)

            def split_h(e):
                need(e, ("x_turn", g), *middle_over)
                return e.activation(t_h[:, :, cols], view, ACT.Copy)
            add("act", ("t_h", g), split_h)

            def split_l(e):
                need(e, ("t_h", g), *middle_over)
                return e.tensor_tensor(t_l[:, :, cols], view, f32(t_h[:, :, cols]), ALU.subtract)
            add("dve", ("t_l", g), split_l)

        route_bank = {}

        def route(g):
            if g % 2 == 0:
                route_bank[g // 2] = take_m_bank(("logits", g // 2))
            dst, before = route_bank[g // 2]
            cols, at = slice(g * P, (g + 1) * P), g % 2 * 2 * NE

            def logits_mm(e):
                need(e, ("t_l", g), "rt_l", before)
                for k in range(KC):
                    for m, t in enumerate((t_h, t_l)):
                        last = e.matmul(dst[:, at:at + 2 * NE], t[:, k, cols], rt_w[:, k, :],
                                        start=(k == 0 and m == 0), stop=(k == KC - 1 and m == 1))
                return last
            add("pe", ("route", g), logits_mm)

        def choose(p):
            r = p % 2
            dst = route_bank[p][0][:].rearrange("p (t h n) -> p t h n", h=2, n=NE)
            logits_v, neg_max = lg[:, r, :, 0:NE], sm[:, r, 0, :]

            def low_half(e):
                need(e, ("route", 2 * p + 1))
                if p >= 2:
                    need(e, ("probs", p - 2))
                return e.activation(ex[:, r], dst[:, :, 1, :], ACT.Copy)
            add("act", ("lg_l", p), low_half)

            def logits(e):
                need(e, ("lg_l", p))
                if p >= 2:
                    need(e, ("coeff", p - 2))
                return e.tensor_tensor(logits_v, dst[:, :, 0, :], ex[:, r], ALU.add)
            fill(("logits", p), logits)

            def largest_logit(e):
                need(e, ("logits", p))
                return e.tensor_reduce(neg_max, logits_v, AX.X, ALU.max, negate=True)
            fill(("neg_max", p), largest_logit)

        def choose_rest(p):
            r = p % 2
            probs_v = lg[:, r, :, 0:NE]
            col = lambda i: sm[:, r, i, :]
            neg_max, total, inv_total, top_total, top_eps, inv_top, half_inv = (col(i) for i in range(7))
            settle(("neg_max", p))

            def expo(e):
                need(e, ("neg_max", p))
                for t in range(2):
                    last = e.activation(ex[:, r, t, :], lg[:, r, t, 0:NE], ACT.Exp, bias=neg_max[:, t:t + 1],
                                        accum_out=total[:, t:t + 1])
                return last
            add("act", ("router_exp", p), expo)

            def inv(e):
                need(e, ("router_exp", p))
                return e.reciprocal(inv_total, total)
            fill(("rsum", p), inv)

            def probs(e):
                need(e, ("rsum", p))
                return e.tensor_tensor(probs_v, ex[:, r], inv_total.unsqueeze(2).broadcast_to([P, 2, NE]),
                                       ALU.mult)
            fill(("probs", p), probs)

            def largest(e):
                need(e, ("probs", p))
                for t in range(2):
                    last = e.max(top[:, r, t, :], lg[:, r, t, 0:NE])
                return last
            fill(("top", p), largest)

            def four(e):
                need(e, ("top", p), "sentinels")
                return e.tensor_copy(top4[:, r, :, 0:TOPK], top[:, r, :, 0:TOPK])
            fill(("top4", p), four)

            def top_sum(e):
                need(e, ("top", p))
                return e.tensor_reduce(top_total, top[:, r, :, 0:TOPK], AX.X, ALU.add)
            fill(("top_sum", p), top_sum)

            def others(e):
                need(e, ("top4", p))
                if p >= 2:
                    need(e, ("cf_turn", p - 2))
                for t in range(2):
                    last = e.match_replace(cf[:, r, t, :], top4[:, r, t, :], lg[:, r, t, :], 0.0)
                return last
            fill(("others", p), others)

            def plus_eps(e):
                need(e, ("top_sum", p))
                return e.tensor_scalar(top_eps, top_total, EPS_FFN, None, ALU.add)
            fill(("top_eps", p), plus_eps)

            def coeff(e):
                need(e, ("others", p))
                return e.tensor_tensor(cf[:, r, :, 0:NE], probs_v, cf[:, r, :, 0:NE], ALU.subtract)
            fill(("coeff", p), coeff)

            def top_inv(e):
                need(e, ("top_eps", p))
                if p >= 2:
                    need(e, ("wt", p - 2))
                return e.reciprocal(inv_top, top_eps)
            fill(("top_inv", p), top_inv)

            def half(e):
                need(e, ("top_inv", p))
                return e.tensor_scalar(half_inv, inv_top, 0.5, None, ALU.mult)
            fill(("half_inv", p), half)

        def turn_choice(p):
            r = p % 2
            settle(("coeff", p))
            dst, before = take(f_items, f_bank, ("cf_t", p))

            def turn(e):
                need(e, ("coeff", p), before)
                for t in range(2):
                    last = e.transpose(dst[:, t * P:(t + 1) * P], cf[:, r, t, 0:NE], ident[:])
                return last
            add("pe", ("cf_turn", p), turn)

            def evacuate(e):
                need(e, ("cf_turn", p))
                if p >= 2:
                    need(e, ("mix", p - 2))
                return e.activation(cf_t[:, r], dst[:, 0:2 * P].rearrange("p (t n) -> p t n", n=P), ACT.Copy)
            add("act", ("cf_t", p), evacuate)

        def mix_weights(p):
            r = p % 2
            dst2, before2 = take_m_bank(("wt", p))

            def mix(e):
                need(e, ("cf_t", p), "mixs", before2)
                for t in range(2):
                    last = e.matmul(dst2[:, t * NK:(t + 1) * NK], cf_t[:, r, t, :], mixs[:], start=True,
                                    stop=True)
                return last
            add("pe", ("mix", p), mix)

            def scaled(e):
                need(e, ("mix", p), ("half_inv", p), *middle_over)
                return e.tensor_tensor(wt[:, 2 * p:2 * p + 2, :],
                                       dst2[:, 0:2 * NK].rearrange("p (t k) -> p t k", k=NK),
                                       sm[:, r, 6, :].unsqueeze(2).broadcast_to([P, 2, NK]), ALU.mult)
            fill(("wt", p), scaled)

        def unit(w, g):
            n = len(g_items) - 4
            r = n % 2
            dst, before = take(g_items, g_bank, ("gb", w, g))
            cols = slice(g * P, (g + 1) * P)
            gate, up = dst[:, 0:I], dst[:, I:2 * I]
            shared = w >= NK

            w_h, w_l = w_hs[w % 2], w_ls[w % 2]

            def mm(e):
                need(e, ("t_l", g), (("w", w), "l", KC - 1))
                need(e, before)
                for k in range(KC):
                    for m, (t, ww) in enumerate(((t_h, w_h), (t_h, w_l), (t_l, w_h))):
                        last = e.matmul(dst[:, 0:2 * I], t[:, k, cols], ww[:, k, :],
                                        start=(k == 0 and m == 0), stop=(k == KC - 1 and m == 2))
                return last
            add("pe", ("unit", w, g), mm)
            two_before = g_items[n + 2] if n >= 2 else None

            def tanh(e):
                need(e, ("unit", w, g))
                if n >= 2:
                    need(e, ("ga",) + two_before[1:])
                return e.activation(th[:, r, :], gate, ACT.Tanh, scale=0.5)
            add("act", ("th", w, g), tanh)

            def first(e):
                need(e, ("th", w, g))
                return e.scalar_tensor_tensor(ga[:, r, :], th[:, r, :], 1.0, up, ALU.add, ALU.mult)
            add("dve", ("ga", w, g), first)

            if shared:
                to = hs[:, g % 2, (w - NK) * I:(w - NK + 1) * I]
            elif w == 0:
                to = macc[:, g, :]
            else:
                to = gb[:, r, :]

            def second(e):
                need(e, ("ga", w, g))
                if shared:
                    if g >= 2:
                        need(e, ("d_turn", g - 2))
                    scale = 0.5
                else:
                    need(e, ("wt", g // 2), *late_over)
                    scale = wt[:, g, w:w + 1]
                    if w > 0 and two_before and two_before[1] > 0:
                        need(e, ("acc",) + two_before[1:])
                return e.scalar_tensor_tensor(to, ga[:, r, :], scale, gate, ALU.mult, ALU.mult)
            add("dve", ("gb", w, g), second)

            if not shared and w > 0:
                def accumulate(e):
                    need(e, ("gb", w, g), ("gb", 0, g))
                    if w > 1:
                        need(e, ("acc", w - 1, g))
                    return e.tensor_tensor(macc[:, g, :], macc[:, g, :], gb[:, r, :], ALU.add)
                add("pool", ("acc", w, g), accumulate)

        def turn_down(g):
            r = g % 2
            blocks = [("m", k) for k in range(I // P)] + [("s", k) for k in range(NS * I // P)]
            for half in range(2):
                part = blocks[half * 3:half * 3 + 3]
                dst, before = take(f_items, f_bank, ("d_l", g, half))

                def turn(e, part=part, dst=dst, before=before):
                    need(e, ("gb", NW - 1, g), ("gb", NW - 2, g), ("acc", NK - 1, g))
                    need(e, before)
                    for i, (kind, k) in enumerate(part):
                        src = macc[:, g, k * P:(k + 1) * P] if kind == "m" else hs[:, r, k * P:(k + 1) * P]
                        last = e.transpose(dst[:, i * P:(i + 1) * P], src, ident[:])
                    return last
                name = ("d_turn", g) if half else ("d_turn0", g)
                add("pe", name, turn)
                view = dst[:, 0:3 * P].rearrange("p (k n) -> p k n", n=P)
                rows = slice(half * 3, half * 3 + 3)

                def split_h(e, name=name, view=view, rows=rows):
                    need(e, name)
                    if g >= 2:
                        need(e, ("down", g - 2))
                    return e.activation(d_h[:, r, rows, :], view, ACT.Copy)
                add("act", ("d_h", g, half), split_h)

                def split_l(e, half=half, view=view, rows=rows):
                    need(e, ("d_h", g, half))
                    if g >= 2:
                        need(e, ("down", g - 2))
                    return e.tensor_tensor(d_l[:, r, rows, :], view, f32(d_h[:, r, rows, :]), ALU.subtract)
                add("dve", ("d_l", g, half), split_l)

        def down(g):
            r = g % 2
            dst, before = take_m_bank(("done", g))
            weights = ([(wd_h[:, k, :], wd_l[:, k, :]) for k in range(I // P)]
                       + [(ws_h[:, k, :], ws_l[:, k, :]) for k in range(NS * I // P)])

            def mm(e):
                need(e, ("d_l", g, 1), ("d_l", g, 0), ("wd", "l", I // P - 1),
                     ("ws", "l", NS * I // P - 1), before)
                for k, (wh, wl) in enumerate(weights):
                    for m, (dd, ww) in enumerate(((d_h, wh), (d_h, wl), (d_l, wh))):
                        last = e.matmul(dst[:], dd[:, r, k, :], ww, start=(k == 0 and m == 0),
                                        stop=(k == ND - 1 and m == 2))
                return last
            add("pe", ("down", g), mm)

            def finish(e):
                need(e, ("down", g))
                return e.tensor_tensor(x1[:, g, :], x1[:, g, :], dst[:], ALU.add)
            add("dve", ("done", g), finish)

            def store(e, s):
                need(e, ("done", g))
                b, t = g // TT, g % TT
                e.dma_start(out[b, t * P:(t + 1) * P, :], x1[:, g, :]).then_inc(s, 16)
            plan.load(("stored", g), f"out{g % 2}", 1, store)

        aliases = {}
        plain_need = plan.need

        def need_with_aliases(engine, *names):
            for name in names:
                for real in aliases.get(name, [name]):
                    plain_need(engine, real)
        need = need_with_aliases

        constants()
        load_batch(0, "ctx")
        load_batch(0, "x")
        plan.load("tables_in", "consts", 4, load_constants)
        load_batch(1, "ctx")
        load_batch(1, "x")
        mixture_table("load")
        output_weights("load")

        def in_tick(n, step):
            ahead, low, product = n + LEAD, n - BEHIND["low_part"], n - BEHIND["value_product"]
            if step in ("scores_x", "scores_y") and 0 <= n < NH:
                pass_b(n, step[-1])
            elif step in ("low_x", "low_y") and 0 <= low < NH:
                low_part(low, step[-1])
            elif step == "value_product" and 0 <= product < NH:
                value_product(product)
            elif step == "value_rows" and 0 <= product < NH:
                value_rows(product)
            elif step[:-1] == "pass_a_" and 0 <= ahead < NH:
                pass_a(ahead, int(step[-1]))
            elif step[:-1] == "row_max_" and 0 <= ahead < NH:
                row_max(ahead, int(step[-1]))
            elif step[:-1] == "fill_pe_":
                fill_pe(int(step[-1]))
            elif step[:-1] == "fill_dve_":
                for _ in range(int(step[-1])):
                    fill_gap(1 + (len(queue) > BACKLOG))

        def ffn_tick(tick):
            if tick == FFN_TAIL["turn_out"]:
                turn_out(NC - 1)
            for g in range(NT - TT, NT):
                if tick == FFN_TAIL["project"] + g % TT:
                    for k in range(KC):
                        project(g, k)
                    moments2(g)
                    if g == NT - 1:
                        norm_scales(B - 1)

            def on(step, pair=False):
                at = tick + FFN_AHEAD[step.__name__]
                if pair and at % 2 == 0 and 0 <= at < NT:
                    step(at // 2)
                if not pair and 0 <= at < NT:
                    step(at)
            on(normalize)
            on(turn_x)
            fill_gap(3)
            on(route)
            on(choose, True)
            on(choose_rest, True)
            fill_gap(2)
            on(turn_choice, True)
            fill_gap(9)
            if 0 <= tick < NT:
                settle(("wt", tick // 2))
                unit(0, tick)
            fill_gap(5)
            on(mix_weights, True)
            fill_gap(4)
            if tick == 1:
                chunk_weights(1)

        for n in range(-20, NH + FFN_START + FFN_LEAD + NT):
            busy = -LEAD <= n < NH
            for c in range(NC):
                if n == c * G + AT["maxima_turned"] + (FIRST_MAXIMA if c == 0 else 0):
                    pe_queue.append(lambda c=c: maxima(c, "turn"))
            for step in TICK:
                in_tick(n, step)
            if not busy and n < NH + FFN_START:
                fill_pe(len(pe_queue))
                fill_gap(len(queue))
            for c in range(NC):
                if n == c * G + AT["maxima_split"]:
                    maxima(c, "split")
            for b in range(B):
                first = b * KV * G
                if b >= 2 and n == first - 20:
                    load_batch(b, "ctx")
                    load_batch(b, "x")
                if n == max(first + AT["key_squares"], -16):
                    key_squares(b)
                if n == max(first + AT["moments"], -16):
                    moments(b)
                if n == first + AT["key_scale"]:
                    key_scale(b)
                if n == first + AT["query_scale"]:
                    query_scale(b)
                if n == first + AT["center"]:
                    center_x(b)
                if n == first + AT["rope_keys"]:
                    rope(b, 0)
                if n == first + AT["values"]:
                    values(b)
                if n == first + AT["turn_keys"]:
                    pe_queue.append(lambda b=b: turn_in(b, 0))
            for c in range(NC):
                b, i = c // KV, c % KV + 1
                if n == c * G + AT["rope_queries"]:
                    rope(b, i)
                if n == c * G + AT["turn_queries"] + (LATER_TURN if c == 1 else 0):
                    pe_queue.append(lambda b=b, i=i: turn_in(b, i))
            for g in range(NT - TT):
                if n == (g // TT + 1) * KV * G + AT["project"] + g % TT:
                    for k in range(KC):
                        pe_queue.append(lambda g=g, k=k: project(g, k))
            for c in range(NC):
                if n == c * G + AT["combine"]:
                    combine(c)
                if n == c * G + AT["turn_out"] + (c % KV == 0) and c < NC - 1:
                    pe_queue.append(lambda c=c: turn_out(c))
            if n == NH - LEAD + 1:
                mixture_table("compute")
            if n == AT["chunk_weights"]:
                chunk_weights(0)
            if n == AT["router_weights"]:
                router_weights()
                sentinels()
            for g in range(NT - TT):
                if n == AT["moments2"] + g // TT:
                    moments2(g)
                    if g % TT == TT - 1:
                        norm_scales(g // TT)
            if n >= NH + FFN_START:
                ffn_tick(n - NH - FFN_START - FFN_LEAD)
            if AT["output_weights"] <= n < AT["output_weights"] + KC:
                pe_queue.append(lambda k=n - AT["output_weights"]: output_weights(k))

        fill_pe(len(pe_queue))
        fill_gap(len(queue))
        for w in range(1, NK):
            for g in range(NT):
                unit(w, g)
                if g == 1:
                    chunk_weights(w + 1)
                if g == 8 and w == 1:
                    down_weights()
        chunk_weights(NK + 1)
        for g in range(-1, NT + 1):
            if g + 1 < NT:
                unit(NK, g + 1)
            if 0 <= g < NT:
                for w in range(NK + 1, NW):
                    unit(w, g)
            if g >= 1:
                down(g - 1)
            if 0 <= g < NT:
                turn_down(g)

        def finish_all(e, s):
            need(e, ("stored", NT - 1), ("stored", NT - 2))
        plan.load("end", "out0", 0, finish_all)

        with nc.Block() as block:
            @block.sync
            def _(e):
                plan.run("sp", e)

            @block.gpsimd
            def _(e):
                plan.run("pool", e)

            @block.scalar
            def _(e):
                plan.run("act", e)

            @block.vector
            def _(e):
                plan.run("dve", e)

            @block.tensor
            def _(e):
                plan.run("pe", e)


_INS = ["x", "ctx_512", "L0_xattn_q_norm_w", "L0_xattn_k_norm_w", "L0_xattn_w_out", "L0_ffn_w_router",
        "L0_ffn_w_gate", "L0_ffn_w_up", "L0_ffn_w_down", "L0_ffn_amplitudes", "L0_ffn_expert_scale",
        "L0_ffn_shared_w_gate", "L0_ffn_shared_w_up", "L0_ffn_shared_w_down"]


def _rope_tables(length, width):
    import numpy as np
    exponent = np.arange(0, width, 2, dtype=np.float32) / np.float32(width)
    inv_freq = (np.float32(1.0) / np.power(np.float32(10000.0), exponent)).astype(np.float32)
    freqs = np.outer(np.arange(length, dtype=np.float32), inv_freq).astype(np.float32)
    cos, sin = np.cos(freqs), np.sin(freqs)
    return (np.concatenate([cos, cos], -1).astype(np.float32),
            np.concatenate([-sin, sin], -1).astype(np.float32))


def kernel(**inputs):
    import numpy as np
    import concourse.bacc as bacc
    from concourse.bass_utils import run_bass_kernel_spmd

    nc = bacc.Bacc("TRN2", target_bir_lowering=False, num_devices=1)
    arrays, args = {}, []
    given = [(name, np.ascontiguousarray(inputs[name])) for name in _INS]
    cos, sin = _rope_tables(512, 32)
    for name, a in given + [("rope_cos", cos), ("rope_sin", sin)]:
        arrays[f"in_{name}"] = a
        args.append(nc.dram_tensor(f"in_{name}", a.shape, mybir.dt.from_np(a.dtype),
                                   kind="ExternalInput").ap())
    shape = given[0][1].shape
    args.append(nc.dram_tensor("out", shape, mybir.dt.float32, kind="ExternalOutput").ap())
    attention_and_mixture_kernel(nc, *args)
    r = run_bass_kernel_spmd(nc, [arrays], core_ids=[0])
    return r.results[0]["out"]
```
